# Optimizing a Trainium2 kernel written in Bass

```python
import numpy as np
import jax
import jax.numpy as jnp

def _softmax(x, axis=-1):
    return jax.nn.softmax(x, axis=axis)

def _gelu(x):
    return jax.nn.gelu(x, approximate=True)

def _silu(x):
    return jax.nn.silu(x)

def _sigmoid(x):
    return jax.nn.sigmoid(x)

def _layernorm(x, axis=-1, eps=1e-05):
    m = jnp.mean(x, axis=axis, keepdims=True)
    v = jnp.var(x, axis=axis, keepdims=True)
    return (x - m) / jnp.sqrt(v + eps)

def _scatter_add(tgt, idx, src, axis=0):
    return tgt.at[idx].add(src)

def _segment_sum(src, seg, n):
    return jax.ops.segment_sum(src, seg, n)
kernel_name = 'mk_xattn_seq_d2_seqx_r8_eceae7'

def setup_inputs(seed: int=0):
    np.random.seed(seed)
    _w = jnp.asarray

    def _rec_inputs():
        import jax
        import jax.numpy as jnp
        _rk = jax.random.key(seed)
        x = -0.0002928 + 1 * jax.random.normal(jax.random.fold_in(_rk, 1), (32, 64, 256), jnp.float32)
        _lenS = 64 - jax.random.randint(jax.random.fold_in(_rk, 7), (32,), 0, max(1, 64 // 4) + 1, jnp.int32)
        _lenS2 = 64 - jax.random.randint(jax.random.fold_in(_rk, 8), (32,), 0, max(1, 64 // 4) + 1, jnp.int32)
        _ctx_2048P = jax.random.normal(jax.random.fold_in(_rk, 11), (32, 16, 256), jnp.float32)
        _ctx_2048c = jax.random.dirichlet(jax.random.fold_in(_rk, 511), 0.3 * jnp.ones((16,), jnp.float32), (32, 64))
        _ctx_2048t = jnp.einsum('bsk,bkd->bsd', _ctx_2048c, _ctx_2048P)
        _ctx_2048t = _ctx_2048t * jax.lax.rsqrt(jnp.mean(jnp.square(_ctx_2048t)) + 1e-12) * 0.953939
        ctx_2048 = -1.39393e-06 + 0.999914 * (_ctx_2048t + 0.3 * jax.random.normal(jax.random.fold_in(_rk, 611), (32, 64, 256), jnp.float32))
        return (x, ctx_2048)
    x, ctx_2048 = _rec_inputs()

    def _L0_xattn_setup():
        import jax, jax.numpy as jnp
        import numpy as np
        N, C, S, S2, H, CTX = (4, 64, 256, 256, 8, 64)
        EPS = 1e-05
        key = jax.random.key(seed)
        ks = jax.random.split(key, 6)
        sd = lambda fan: 1.0 / np.sqrt(fan)
        return {'input': jax.random.normal(ks[0], (N, C, S), jnp.float32), 'context': jax.random.normal(ks[1], (N, CTX, S2), jnp.float32), 'gamma': jnp.ones((C,), jnp.float32), 'beta': jnp.zeros((C,), jnp.float32), 'Wq': jax.random.normal(ks[2], (C * H, C), jnp.float32) * sd(C), 'bq': jnp.zeros((C * H,), jnp.float32), 'Wkv': jax.random.normal(ks[3], (C * H * 2, CTX), jnp.float32) * sd(CTX), 'bkv': jnp.zeros((C * H * 2,), jnp.float32), 'Wo': jax.random.normal(ks[4], (C, C * H), jnp.float32) * sd(C * H), 'bo': jnp.zeros((C,), jnp.float32)}
    _L0_xattn_all = _L0_xattn_setup()
    _L0_xattn_in = {k: v for k, v in _L0_xattn_all.items() if k in ('gamma', 'beta', 'Wq', 'bq', 'Wkv', 'bkv', 'Wo', 'bo')}
    del _L0_xattn_all

    def _L1_xattn_setup():
        import jax, jax.numpy as jnp
        import numpy as np
        N_HEAD = 32
        EPS = 1e-05

        def _ln(x, w, b):
            m = jnp.mean(x, axis=-1, keepdims=True)
            v = jnp.mean((x - m) ** 2, axis=-1, keepdims=True)
            return (x - m) * jax.lax.rsqrt(v + EPS) * w + b

        def _forward(x, state, i, ln1_w, ln1_b, ln2_w, ln2_b, maa_x, maa_w, maa_k, maa_v, maa_r, maa_g, maa_w1, maa_w2, time_decay, decay_w1, decay_w2, faaaa, Wr, Wk, Wv, Wg, Wo, gn_w, gn_b, fmaa_k, fmaa_r, fWk, fWr, fWv):
            B, L, C = x.shape
            H = N_HEAD
            S = C // H
            i0 = (2 + S) * i
            xa = _ln(x, ln1_w, ln1_b)
            sx = jnp.concatenate([state[:, i0 + 1][:, None], xa[:, :-1]], axis=1) - xa
            xxx = xa + sx * maa_x
            t = jnp.tanh(xxx @ maa_w1).reshape(B, L, 5, -1)
            m = jnp.einsum('blfd,fdc->blfc', t, maa_w2)
            mw, mk, mv, mr, mg = (m[:, :, j] for j in range(5))
            xw = xa + sx * (maa_w + mw)
            xk = xa + sx * (maa_k + mk)
            xv = xa + sx * (maa_v + mv)
            xr = xa + sx * (maa_r + mr)
            xg = xa + sx * (maa_g + mg)
            w = time_decay + jnp.tanh(xw @ decay_w1) @ decay_w2
            w = jnp.exp(-jnp.exp(w)).reshape(B, L, H, S)
            r = (xr @ Wr.T).reshape(B, L, H, S)
            k = (xk @ Wk.T).reshape(B, L, H, S)
            v = (xv @ Wv.T).reshape(B, L, H, S)
            g = jax.nn.silu(xg @ Wg.T)
            s0 = state[:, i0 + 2:i0 + 2 + S].reshape(B, H, S, S)

            def step(s, inp):
                k_l, v_l, w_l, r_l = inp
                a = k_l[..., :, None] * v_l[..., None, :]
                out = jnp.einsum('bhs,bhst->bht', r_l, faaaa * a + s)
                s_new = a + w_l[..., None] * s
                return (s_new, out)
            seq = tuple((z.transpose(1, 0, 2, 3) for z in (k, v, w, r)))
            _, outs = jax.lax.scan(step, s0, seq)
            y = outs.transpose(1, 0, 2, 3)
            gm = jnp.mean(y, axis=-1, keepdims=True)
            gv = jnp.mean((y - gm) ** 2, axis=-1, keepdims=True)
            y = ((y - gm) * jax.lax.rsqrt(gv + EPS)).reshape(B, L, C) * gn_w + gn_b
            x = x + y * g @ Wo.T
            xc = _ln(x, ln2_w, ln2_b)
            sxc = jnp.concatenate([state[:, i0][:, None], xc[:, :-1]], axis=1) - xc
            xk2 = xc + sxc * fmaa_k
            xr2 = xc + sxc * fmaa_r
            rr = jax.nn.sigmoid(xr2 @ fWr.T)
            kk = jnp.square(jax.nn.relu(xk2 @ fWk.T))
            x = x + rr * (kk @ fWv.T)
            return x
        key = jax.random.key(seed)
        B, L, C, H = (8, 64, 256, N_HEAD)
        S = C // H
        DM, DD = (32, 64)
        ks = jax.random.split(key, 32)
        n = lambda k, shp, s=1.0: jax.random.normal(k, shp, dtype=jnp.float32) * s
        u = lambda k, shp: jax.random.uniform(k, shp, dtype=jnp.float32)
        inp = {'x': n(ks[0], (B, L, C)), 'state': n(ks[1], (B, 2 + S, C), 0.1), 'i': 0, 'ln1_w': jnp.ones((C,), jnp.float32), 'ln1_b': jnp.zeros((C,), jnp.float32), 'ln2_w': jnp.ones((C,), jnp.float32), 'ln2_b': jnp.zeros((C,), jnp.float32), 'maa_x': u(ks[2], (C,)), 'maa_w': u(ks[3], (C,)), 'maa_k': u(ks[4], (C,)), 'maa_v': u(ks[5], (C,)), 'maa_r': u(ks[6], (C,)), 'maa_g': u(ks[7], (C,)), 'maa_w1': n(ks[8], (C, 5 * DM), 0.02), 'maa_w2': n(ks[9], (5, DM, C), 0.02), 'time_decay': n(ks[10], (C,), 0.5), 'decay_w1': n(ks[11], (C, DD), 0.02), 'decay_w2': n(ks[12], (DD, C), 0.02), 'faaaa': n(ks[13], (H, S, 1), 0.1), 'Wr': n(ks[14], (C, C), 0.02), 'Wk': n(ks[15], (C, C), 0.02), 'Wv': n(ks[16], (C, C), 0.02), 'Wg': n(ks[17], (C, C), 0.02), 'Wo': n(ks[18], (C, C), 0.02), 'gn_w': jnp.ones((C,), jnp.float32), 'gn_b': jnp.zeros((C,), jnp.float32), 'fmaa_k': u(ks[19], (C,)), 'fmaa_r': u(ks[20], (C,)), 'fWk': n(ks[21], (C, C), 0.02), 'fWr': n(ks[22], (C, C), 0.02), 'fWv': n(ks[23], (C, C), 0.02)}
        return inp
    _L1_xattn_all = _L1_xattn_setup()
    _L1_xattn_in = {k: v for k, v in _L1_xattn_all.items() if k in ('ln1_w', 'ln1_b', 'ln2_w', 'ln2_b', 'maa_x', 'maa_w', 'maa_k', 'maa_v', 'maa_r', 'maa_g', 'maa_w1', 'maa_w2', 'time_decay', 'decay_w1', 'decay_w2', 'faaaa', 'Wr', 'Wk', 'Wv', 'Wg', 'Wo', 'gn_w', 'gn_b', 'fmaa_k', 'fmaa_r', 'fWk', 'fWr', 'fWv')}
    del _L1_xattn_all
    return {'x': x, 'ctx_2048': ctx_2048, 'L0_xattn_gamma': _L0_xattn_in['gamma'], 'L0_xattn_beta': _L0_xattn_in['beta'], 'L0_xattn_Wq': _L0_xattn_in['Wq'], 'L0_xattn_bq': _L0_xattn_in['bq'], 'L0_xattn_Wkv': _L0_xattn_in['Wkv'], 'L0_xattn_bkv': _L0_xattn_in['bkv'], 'L0_xattn_Wo': _L0_xattn_in['Wo'], 'L0_xattn_bo': _L0_xattn_in['bo'], 'L1_xattn_ln1_w': _L1_xattn_in['ln1_w'], 'L1_xattn_ln1_b': _L1_xattn_in['ln1_b'], 'L1_xattn_ln2_w': _L1_xattn_in['ln2_w'], 'L1_xattn_ln2_b': _L1_xattn_in['ln2_b'], 'L1_xattn_maa_x': _L1_xattn_in['maa_x'], 'L1_xattn_maa_w': _L1_xattn_in['maa_w'], 'L1_xattn_maa_k': _L1_xattn_in['maa_k'], 'L1_xattn_maa_v': _L1_xattn_in['maa_v'], 'L1_xattn_maa_r': _L1_xattn_in['maa_r'], 'L1_xattn_maa_g': _L1_xattn_in['maa_g'], 'L1_xattn_maa_w1': _L1_xattn_in['maa_w1'], 'L1_xattn_maa_w2': _L1_xattn_in['maa_w2'], 'L1_xattn_time_decay': _L1_xattn_in['time_decay'], 'L1_xattn_decay_w1': _L1_xattn_in['decay_w1'], 'L1_xattn_decay_w2': _L1_xattn_in['decay_w2'], 'L1_xattn_faaaa': _L1_xattn_in['faaaa'], 'L1_xattn_Wr': _L1_xattn_in['Wr'], 'L1_xattn_Wk': _L1_xattn_in['Wk'], 'L1_xattn_Wv': _L1_xattn_in['Wv'], 'L1_xattn_Wg': _L1_xattn_in['Wg'], 'L1_xattn_Wo': _L1_xattn_in['Wo'], 'L1_xattn_gn_w': _L1_xattn_in['gn_w'], 'L1_xattn_gn_b': _L1_xattn_in['gn_b'], 'L1_xattn_fmaa_k': _L1_xattn_in['fmaa_k'], 'L1_xattn_fmaa_r': _L1_xattn_in['fmaa_r'], 'L1_xattn_fWk': _L1_xattn_in['fWk'], 'L1_xattn_fWr': _L1_xattn_in['fWr'], 'L1_xattn_fWv': _L1_xattn_in['fWv']}

def reference(x, ctx_2048, L0_xattn_gamma, L0_xattn_beta, L0_xattn_Wq, L0_xattn_bq, L0_xattn_Wkv, L0_xattn_bkv, L0_xattn_Wo, L0_xattn_bo, L1_xattn_ln1_w, L1_xattn_ln1_b, L1_xattn_ln2_w, L1_xattn_ln2_b, L1_xattn_maa_x, L1_xattn_maa_w, L1_xattn_maa_k, L1_xattn_maa_v, L1_xattn_maa_r, L1_xattn_maa_g, L1_xattn_maa_w1, L1_xattn_maa_w2, L1_xattn_time_decay, L1_xattn_decay_w1, L1_xattn_decay_w2, L1_xattn_faaaa, L1_xattn_Wr, L1_xattn_Wk, L1_xattn_Wv, L1_xattn_Wg, L1_xattn_Wo, L1_xattn_gn_w, L1_xattn_gn_b, L1_xattn_fmaa_k, L1_xattn_fmaa_r, L1_xattn_fWk, L1_xattn_fWr, L1_xattn_fWv):
    import jax
    import jax.numpy as jnp

    def _L0_xattn_ref(input, context, gamma, beta, Wq, bq, Wkv, bkv, Wo, bo):
        import jax, jax.numpy as jnp
        import numpy as np
        N, C, S, S2, H, CTX = (4, 64, 256, 256, 8, 64)
        EPS = 1e-05
        n, c, s = input.shape
        h = H
        mu = jnp.mean(input, axis=(1, 2), keepdims=True)
        var = jnp.var(input, axis=(1, 2), keepdims=True)
        xn = (input - mu) * jax.lax.rsqrt(var + EPS)
        xn = xn * gamma[None, :, None] + beta[None, :, None]
        q = jnp.einsum('oc,ncs->nos', Wq, xn) + bq[None, :, None]
        kv = jnp.einsum('od,nds->nos', Wkv, context) + bkv[None, :, None]
        q = q.reshape(n, h, c, s).transpose(0, 1, 3, 2)
        kv = kv.reshape(n, 2 * h, c, -1).transpose(0, 1, 3, 2)
        k, v = (kv[:, :h], kv[:, h:])
        scale = c ** (-0.25)
        att = jax.nn.softmax(jnp.einsum('nhqc,nhkc->nhqk', q * scale, k * scale), axis=-1)
        y = jnp.einsum('nhqk,nhkc->nhqc', att, v)
        y = y.transpose(0, 1, 3, 2).reshape(n, h * c, s)
        out = jnp.einsum('co,nos->ncs', Wo, y) + bo[None, :, None]
        return input + out

    def _L1_xattn_ref(x, state, i, ln1_w, ln1_b, ln2_w, ln2_b, maa_x, maa_w, maa_k, maa_v, maa_r, maa_g, maa_w1, maa_w2, time_decay, decay_w1, decay_w2, faaaa, Wr, Wk, Wv, Wg, Wo, gn_w, gn_b, fmaa_k, fmaa_r, fWk, fWr, fWv):
        import jax, jax.numpy as jnp
        import numpy as np
        N_HEAD = 32
        EPS = 1e-05

        def _ln(x, w, b):
            m = jnp.mean(x, axis=-1, keepdims=True)
            v = jnp.mean((x - m) ** 2, axis=-1, keepdims=True)
            return (x - m) * jax.lax.rsqrt(v + EPS) * w + b

        def _forward(x, state, i, ln1_w, ln1_b, ln2_w, ln2_b, maa_x, maa_w, maa_k, maa_v, maa_r, maa_g, maa_w1, maa_w2, time_decay, decay_w1, decay_w2, faaaa, Wr, Wk, Wv, Wg, Wo, gn_w, gn_b, fmaa_k, fmaa_r, fWk, fWr, fWv):
            B, L, C = x.shape
            H = N_HEAD
            S = C // H
            i0 = (2 + S) * i
            xa = _ln(x, ln1_w, ln1_b)
            sx = jnp.concatenate([state[:, i0 + 1][:, None], xa[:, :-1]], axis=1) - xa
            xxx = xa + sx * maa_x
            t = jnp.tanh(xxx @ maa_w1).reshape(B, L, 5, -1)
            m = jnp.einsum('blfd,fdc->blfc', t, maa_w2)
            mw, mk, mv, mr, mg = (m[:, :, j] for j in range(5))
            xw = xa + sx * (maa_w + mw)
            xk = xa + sx * (maa_k + mk)
            xv = xa + sx * (maa_v + mv)
            xr = xa + sx * (maa_r + mr)
            xg = xa + sx * (maa_g + mg)
            w = time_decay + jnp.tanh(xw @ decay_w1) @ decay_w2
            w = jnp.exp(-jnp.exp(w)).reshape(B, L, H, S)
            r = (xr @ Wr.T).reshape(B, L, H, S)
            k = (xk @ Wk.T).reshape(B, L, H, S)
            v = (xv @ Wv.T).reshape(B, L, H, S)
            g = jax.nn.silu(xg @ Wg.T)
            s0 = state[:, i0 + 2:i0 + 2 + S].reshape(B, H, S, S)

            def step(s, inp):
                k_l, v_l, w_l, r_l = inp
                a = k_l[..., :, None] * v_l[..., None, :]
                out = jnp.einsum('bhs,bhst->bht', r_l, faaaa * a + s)
                s_new = a + w_l[..., None] * s
                return (s_new, out)
            seq = tuple((z.transpose(1, 0, 2, 3) for z in (k, v, w, r)))
            _, outs = jax.lax.scan(step, s0, seq)
            y = outs.transpose(1, 0, 2, 3)
            gm = jnp.mean(y, axis=-1, keepdims=True)
            gv = jnp.mean((y - gm) ** 2, axis=-1, keepdims=True)
            y = ((y - gm) * jax.lax.rsqrt(gv + EPS)).reshape(B, L, C) * gn_w + gn_b
            x = x + y * g @ Wo.T
            xc = _ln(x, ln2_w, ln2_b)
            sxc = jnp.concatenate([state[:, i0][:, None], xc[:, :-1]], axis=1) - xc
            xk2 = xc + sxc * fmaa_k
            xr2 = xc + sxc * fmaa_r
            rr = jax.nn.sigmoid(xr2 @ fWr.T)
            kk = jnp.square(jax.nn.relu(xk2 @ fWk.T))
            x = x + rr * (kk @ fWv.T)
            return x
        return _forward(x, state, i, ln1_w, ln1_b, ln2_w, ln2_b, maa_x, maa_w, maa_k, maa_v, maa_r, maa_g, maa_w1, maa_w2, time_decay, decay_w1, decay_w2, faaaa, Wr, Wk, Wv, Wg, Wo, gn_w, gn_b, fmaa_k, fmaa_r, fWk, fWr, fWv)
    x = _L0_xattn_ref(x, ctx_2048, L0_xattn_gamma, L0_xattn_beta, L0_xattn_Wq, L0_xattn_bq, L0_xattn_Wkv, L0_xattn_bkv, L0_xattn_Wo, L0_xattn_bo)
    x = _L1_xattn_ref(x, ctx_2048, 0, L1_xattn_ln1_w, L1_xattn_ln1_b, L1_xattn_ln2_w, L1_xattn_ln2_b, L1_xattn_maa_x, L1_xattn_maa_w, L1_xattn_maa_k, L1_xattn_maa_v, L1_xattn_maa_r, L1_xattn_maa_g, L1_xattn_maa_w1, L1_xattn_maa_w2, L1_xattn_time_decay, L1_xattn_decay_w1, L1_xattn_decay_w2, L1_xattn_faaaa, L1_xattn_Wr, L1_xattn_Wk, L1_xattn_Wv, L1_xattn_Wg, L1_xattn_Wo, L1_xattn_gn_w, L1_xattn_gn_b, L1_xattn_fmaa_k, L1_xattn_fmaa_r, L1_xattn_fWk, L1_xattn_fWr, L1_xattn_fWv)
    return x

_drawn_inputs = setup_inputs


def setup_inputs(seed=0):
    import zlib

    import numpy as np

    out = dict(_drawn_inputs(seed))
    spreads = {'L0_xattn_gamma': (1.0, 0.2),
     'L0_xattn_beta': (0.0, 0.293),
     'L0_xattn_bq': (0.0, 0.279),
     'L0_xattn_bkv': (0.0, 0.8),
     'L0_xattn_bo': (0.0, 0.8),
     'L1_xattn_ln1_w': (1.0, 0.6),
     'L1_xattn_ln1_b': (0.0, 0.609),
     'L1_xattn_ln2_w': (1.0, 0.6),
     'L1_xattn_ln2_b': (0.0, 0.8),
     'L1_xattn_gn_w': (1.0, 0.6),
     'L1_xattn_gn_b': (0.0, 0.8)}
    factors = {'L1_xattn_maa_x': 8.0,
     'L1_xattn_maa_w': 8.0,
     'L1_xattn_maa_v': 2.752,
     'L1_xattn_maa_w1': 8.0,
     'L1_xattn_maa_w2': 8.0,
     'L1_xattn_time_decay': 3.729,
     'L1_xattn_decay_w1': 8.0,
     'L1_xattn_decay_w2': 8.0,
     'L1_xattn_faaaa': 7.955,
     'L1_xattn_fmaa_k': 7.71,
     'L1_xattn_fmaa_r': 8.0,
     'L1_xattn_fWk': 4.441,
     'L1_xattn_fWr': 8.0,
     'L1_xattn_fWv': 4.048}
    for name, (base, spread) in spreads.items():
        noise = np.random.default_rng([zlib.crc32(name.encode()), seed]).standard_normal(out[name].shape)
        drawn = base * np.exp(spread * noise) if base else spread * noise
        out[name] = jnp.asarray(drawn.astype(out[name].dtype))
    for name, factor in factors.items():
        out[name] = (out[name] * factor).astype(out[name].dtype)
    return out
```

```python
import numpy as np
import concourse.bass as bass
from concourse import mybir
from concourse.alu_op_type import AluOpType as ALU
from contextlib import ExitStack

FP32 = mybir.dt.float32
ACT = mybir.ActivationFunctionType

B, L, C = 32, 64, 256
P = 128
PAIRS = B // 2
CC = 64
HP = 4
UNITS = 2 * HP
QT = C // P
VW = CC + 1
G = 8
GROUPS = B // G
GT = G * L
TT = GT // P
CT = C // P
HS = 8
MAA = 5
MD = 32
DD = 64
EPS = 1e-5

VECTORS = ["ln1_w", "ln1_b", "ln2_w", "ln2_b", "maa_x", "maa_w", "maa_k", "maa_v", "maa_r", "maa_g",
           "time_decay", "faaaa", "gn_w", "gn_b", "fmaa_k", "fmaa_r"]
SQUARES = ["Wr", "Wk", "Wv", "Wg", "Wo", "fWk", "fWr", "fWv"]

FIELDS = [("wq", HP * P), ("wk", HP * P), ("wv", HP * P), ("wo", HP * CC), ("bq", HP), ("bk", HP), ("bv", HP),
          ("gamma", 1), ("beta", 1), ("bo", 1),
          *[(n, CT) for n in VECTORS],
          ("maa_w1", CT * MAA * MD), ("maa_w2", C), ("maa_w2g", C), ("decay_w1", CT * DD), ("decay_w2", C),
          *[(n, CT * C) for n in SQUARES],
          ("ident", P), ("mean64", P), ("ones8", P), ("mean8", P), ("spread", HS * P), ("gather", HS * P)]


def offsets():
    at, out = 0, {}
    for name, width in FIELDS:
        out[name] = (at, width)
        at += width
    return out, at


OFF, WIDTH = offsets()


def build(nc, x, ctx, params, shift, state, out):
    es = ExitStack()
    with es:
        def sb(name, shape):
            return es.enter_context(nc.sbuf_tensor(name, shape, FP32))

        def sem(name):
            return es.enter_context(nc.semaphore(name))

        params_sb = sb("params_sb", [P, WIDTH])

        def par(name, *dims):
            at, width = OFF[name]
            v = params_sb[:, at:at + width]
            if len(dims) == 2:
                v = v.rearrange("p (a b) -> p a b", a=dims[0])
            return v

        banks = [es.enter_context(nc.psum_tensor(f"bank{b}", [P, 512], FP32)) for b in range(8)]

        X = sb("X", [P, PAIRS, C])
        ctx_all = sb("ctx_all", [P, PAIRS, C])
        shift_sb = sb("shift_sb", [P, 2, CT, B])
        state_sb = sb("state_sb", [P, CT, HS, B])
        eps = sb("eps", [P, 1])

        layer0(nc, sem, par, banks, X, ctx_all, shift_sb, state_sb, eps, params_sb,
               x, ctx, params, shift, state)
        layer1(nc, sem, par, banks, X, shift_sb, state_sb, eps, out)


def wait(eng, semaphore, value):
    if not isinstance(value, int) or value > 0:
        eng.wait_ge(semaphore, value)


def buffers(build_layer):
    def run(nc, *args):
        with ExitStack() as es:
            build_layer(nc, lambda name, shape: es.enter_context(nc.sbuf_tensor(name, shape, FP32)), *args)
    return run


@buffers
def layer0(nc, sb, sem, par, banks, X, ctx_all, shift_sb, state_sb, eps, params_sb, x, ctx, params, shift,
           state):
    wq, wk, wv = par("wq"), par("wk"), par("wv")
    wo = par("wo", HP, CC)
    bq, bk, bv = par("bq"), par("bk"), par("bv")
    ident = par("ident")

    stats = sb("stats", [P, PAIRS, 6])
    moments = sb("moments", [P, PAIRS, 2])
    offset = sb("offset", [P, PAIRS])
    spread = sb("spread_sq", [P, PAIRS])
    lnvar = sb("lnvar", [P, PAIRS])
    gn_scale = sb("gn_scale", [P, PAIRS])
    gn_shift = sb("gn_shift", [P, PAIRS])
    out_bias = sb("out_bias", [P, 1])
    xn = sb("xn", [P, C])
    ct = sb("ct", [P, C])
    qk = sb("qk", [P, UNITS, 2, C])
    v = sb("v", [P, UNITS, QT, 2, VW])
    probs = sb("probs", [P, 2, 2, QT, C])
    neg_max = sb("neg_max", [P, 2, 4])
    pT = sb("pT", [P, 2, QT, C])
    recip = sb("recip", [P, 2, 4])
    y = sb("y", [P, 2, QT, P])
    yT = sb("yT", [P, 2, HP, C])

    scores = [[banks[0], banks[1]], [banks[2], banks[3]]]
    turned = banks[4]
    attn = banks[5][:, 0:2 * QT * VW].rearrange("p (q h c) -> p q h c", q=QT, h=2)
    misc = [banks[6], banks[7]]

    loaded = sem("loaded")
    ctx_loaded = sem("ctx_loaded")
    state_loaded = sem("state_loaded")
    consts_set = sem("consts_set")
    scaled_wq = sem("scaled_wq")
    stats_done = sem("stats_done")
    gn_means = sem("gn_means")
    gn_offsets = sem("gn_offsets")
    gn_vars = sem("gn_vars")
    gn_log = sem("gn_log")
    gn_rstd = sem("gn_rstd")
    gn_affine = sem("gn_affine")
    bias_product = sem("bias_product")
    bias_read = sem("bias_read")
    xn_ready = sem("xn_ready")
    ct_ready = sem("ct_ready")
    scores_ready = sem("scores_ready")
    max_ready = sem("max_ready")
    probs_ready = sem("probs_ready")
    turned_ready = sem("turned_ready")
    pT_ready = sem("pT_ready")
    attn_ready = sem("attn_ready")
    recip_ready = sem("recip_ready")
    y_ready = sem("y_ready")
    misc_full = [sem("misc_full0"), sem("misc_full1")]
    misc_free = [sem("misc_free0"), sem("misc_free1")]
    x1_ready = sem("x1_ready")


    def uses(smp, last):
        names = []
        for u in range(UNITS):
            if u >= 1 and (u - 1) % 2 == smp:
                names.append(("yT", u - 1))
            if not last and u % 2 == 0 and u >= 2:
                names.append(("v", u // 2 - 1))
            if not last and u % 2 == 1:
                names.append(("qk", u // 2))
        if not last:
            names.append(("v", HP - 1))
        if smp == 1:
            names.append(("yT", UNITS - 1))
        if smp == 0:
            names.append(("out", 0))
        return names

    PER_PAIR = [len(uses(s, False)) for s in range(2)]
    PROLOGUE = 2 * HP

    def use(smp, i, last, name):
        return PER_PAIR[smp] * i + PROLOGUE + uses(smp, last).index(name)

    with nc.Block() as block:
        @block.sync
        def _(sp):
            sp.dma_start(params_sb[:, :], params).then_inc(loaded, 16)
            for q in range(4):
                sl = slice(q * PAIRS // 4, (q + 1) * PAIRS // 4)
                sp.dma_start(X[:, sl, :], x[:, sl, :]).then_inc(loaded, 16)
            sp.dma_start(ctx_all[:, :, :], ctx).then_inc(ctx_loaded, 16)
            sp.dma_start(shift_sb[:, :, :, :], shift).then_inc(state_loaded, 16)
            sp.dma_start(state_sb[:, :, :, :], state).then_inc(state_loaded, 16)
            sp.wait_ge(state_loaded, 32)

        @block.gpsimd
        def _(pool):
            nc.gpsimd.memset(v[:, :, :, :, CC:VW], 1.0).then_inc(consts_set, 1)
            nc.gpsimd.memset(eps[:, :], EPS).then_inc(consts_set, 1)
            pool.wait_ge(ctx_loaded, 16)

            def copy_ctx(p):
                if not isinstance(p, int):
                    pool.wait_ge(misc_full[1], PER_PAIR[1] * (p - 1) + PROLOGUE)
                nc.gpsimd.tensor_copy(ct[:, :], ctx_all[:, bass.ds(p, 1), :]).then_inc(ct_ready, 1)

            copy_ctx(0)
            with pool.Fori(0, PAIRS - 1) as i:
                copy_ctx(i + 1)

        @block.vector
        def _(dve):
            def shape3(bank):
                return bank[:, :].rearrange("p (a n) -> p a n", a=2)

            dve.sem_inc(pT_ready, 1)
            dve.sem_inc(y_ready, 1)
            dve.wait_ge(loaded, 16 * 5)
            nc.vector.tensor_scalar(wq, wq, 0.125, None, ALU.mult).then_inc(scaled_wq, 1)
            nc.vector.tensor_scalar(bq, bq, 0.125, None, ALU.mult).then_inc(scaled_wq, 1)
            for p in range(PAIRS):
                nc.vector.bn_stats(stats[:, p, :], X[:, p, :]).then_inc(stats_done, 1)
            for p in range(PAIRS):
                dve.wait_ge(stats_done, p + 1)
                nc.vector.bn_aggr(moments[:, p, :], stats[:, p, :]).then_inc(stats_done, 1)
            mean, var = moments[:, :, 0], moments[:, :, 1]
            dve.wait_ge(stats_done, 2 * PAIRS)
            dve.wait_ge(gn_means, 1)
            nc.vector.tensor_tensor(offset[:, :], mean, misc[0][:, 0:PAIRS], ALU.subtract).then_inc(gn_offsets, 1)
            dve.wait_ge(gn_offsets, 1)
            nc.vector.tensor_tensor(spread[:, :], offset[:, :], offset[:, :], ALU.mult).then_inc(gn_offsets, 1)
            dve.wait_ge(gn_offsets, 2)
            nc.vector.tensor_tensor(spread[:, :], spread[:, :], var, ALU.add).then_inc(gn_offsets, 1)
            dve.wait_ge(gn_rstd, 1)
            nc.vector.tensor_scalar(gn_scale[:, :], lnvar[:, :], par("gamma"), None, ALU.mult).then_inc(gn_affine, 1)
            dve.wait_ge(gn_affine, 1)
            nc.vector.tensor_tensor(offset[:, :], gn_scale[:, :], misc[0][:, 0:PAIRS], ALU.mult).then_inc(gn_affine, 1)
            dve.wait_ge(gn_affine, 2)
            nc.vector.tensor_scalar(gn_shift[:, :], offset[:, :], -1.0, par("beta"), ALU.mult, ALU.add)\
                .then_inc(gn_affine, 1)
            dve.wait_ge(bias_product, 1)
            nc.vector.tensor_tensor(out_bias[:, :], par("bo"), misc[1][:, 0:1], ALU.add).then_inc(bias_read, 1)
            dve.wait_ge(bias_read, 1)
            dve.wait_ge(gn_affine, 3)

            def normalise(p):
                if not isinstance(p, int):
                    dve.wait_ge(misc_full[1], PER_PAIR[1] * (p - 1) + PROLOGUE)
                nc.vector.tensor_scalar(xn[:, :], X[:, bass.ds(p, 1), :], gn_scale[:, bass.ds(p, 1)],
                                        gn_shift[:, bass.ds(p, 1)], ALU.mult, ALU.add).then_inc(xn_ready, 1)

            def row_max(g, u):
                s = u % 2
                dve.wait_ge(scores_ready, g + 1)
                for h in range(2):
                    ins = nc.vector.tensor_reduce(neg_max[:, s, 2 * h:2 * h + 2], shape3(scores[s][h]),
                                                  mybir.AxisListType.X, ALU.max, negate=True)
                ins.then_inc(max_ready, 1)

            def copy_pT(g, h):
                dve.wait_ge(turned_ready, 2 * g + h + 1)
                nc.vector.tensor_copy(pT[:, h, :, :], shape3(turned)).then_inc(pT_ready, 1)

            def divide(g, u):
                s = u % 2
                dve.wait_ge(attn_ready, g + 1)
                r = recip[:, s, :].rearrange("p (q h) -> p q h", q=QT)
                nc.vector.reciprocal(r, attn[:, :, :, CC]).then_inc(recip_ready, 1)
                dve.wait_ge(recip_ready, g + 1)
                nc.vector.tensor_tensor(y[:, s, :, :].rearrange("p q (h c) -> p q h c", h=2), attn[:, :, :, 0:CC],
                                        r.unsqueeze(3).broadcast_to([P, QT, 2, CC]), ALU.mult).then_inc(y_ready, 1)

            normalise(0)
            row_max(0, 0)

            def body(i, last):
                if not last:
                    normalise(i + 1)
                for u in range(UNITS):
                    g = UNITS * i + u
                    copy_pT(g, 0)
                    if not (last and u == UNITS - 1):
                        row_max(g + 1, u + 1)
                    copy_pT(g, 1)
                    divide(g, u)
                dve.wait_ge(misc_full[0], use(0, i, last, ("out", 0)) + 1)
                xi = X[:, bass.ds(i, 1), :].rearrange("p a n -> p (a n)")
                nc.vector.scalar_tensor_tensor(xi, misc[0][:, 0:C], out_bias[:, 0:1], xi, ALU.add, ALU.add)\
                    .then_inc(misc_free[0], 1)

            with dve.Fori(0, PAIRS - 1) as i:
                body(i, False)
            body(PAIRS - 1, True)

        @block.scalar
        def _(act):
            act.sem_inc(probs_ready, 1)
            act.wait_ge(consts_set, 2)
            act.wait_ge(gn_vars, 1)
            nc.scalar.activation(lnvar[:, :], misc[0][:, PAIRS:2 * PAIRS], ACT.Ln, bias=eps[:, 0:1]).then_inc(gn_log, 1)
            act.wait_ge(gn_log, 1)
            nc.scalar.activation(lnvar[:, :], lnvar[:, :], ACT.Exp, scale=-0.5).then_inc(gn_rstd, 1)

            def exps(g, u):
                s = u % 2
                act.wait_ge(max_ready, g + 1)
                for h in range(2):
                    for q in range(QT):
                        n = 2 * h + q
                        nc.scalar.activation(probs[:, s, h, q, :], scores[s][h][:, q * C:(q + 1) * C], ACT.Exp,
                                             bias=neg_max[:, s, n:n + 1]).then_inc(probs_ready, 1)

            def take_qk(smp, hp, n):
                act.wait_ge(misc_full[smp], n + 1)
                u = 2 * hp + smp
                nc.scalar.activation(qk[:, u, 0, :], misc[smp][:, 0:C], ACT.Identity, bias=bq[:, hp:hp + 1])
                nc.scalar.activation(qk[:, u, 1, :], misc[smp][:, C:2 * C], ACT.Identity, bias=bk[:, hp:hp + 1])\
                    .then_inc(misc_free[smp], 1)

            def take_v(smp, hp, n):
                act.wait_ge(misc_full[smp], n + 1)
                u = 2 * hp + smp
                nc.scalar.copy(v[:, u, :, :, 0:CC],
                               misc[smp][:, 0:QT * P].rearrange("p (k h c) -> p k h c", k=QT, h=2))\
                    .then_inc(misc_free[smp], 1)

            def take_yT(u, n):
                smp = u % 2
                act.wait_ge(misc_full[smp], n + 1)
                nc.scalar.copy(yT[:, smp, u // 2, :], misc[smp][:, 0:C]).then_inc(misc_free[smp], 1)

            act.wait_ge(scaled_wq, 2)
            for hp in range(HP):
                for smp in range(2):
                    take_qk(smp, hp, 2 * hp)
                for smp in range(2):
                    take_v(smp, hp, 2 * hp + 1)
            exps(0, 0)

            def body(i, last):
                for u in range(UNITS):
                    g = UNITS * i + u
                    if not (last and u == UNITS - 1):
                        exps(g + 1, u + 1)
                    if u >= 1:
                        take_yT(u - 1, use((u - 1) % 2, i, last, ("yT", u - 1)))
                    if not last and u % 2 == 0 and u >= 2:
                        for smp in range(2):
                            take_v(smp, u // 2 - 1, use(smp, i, last, ("v", u // 2 - 1)))
                    if not last and u % 2 == 1:
                        for smp in range(2):
                            take_qk(smp, u // 2, use(smp, i, last, ("qk", u // 2)))
                if not last:
                    for smp in range(2):
                        take_v(smp, HP - 1, use(smp, i, last, ("v", HP - 1)))
                take_yT(UNITS - 1, use(1, i, last, ("yT", UNITS - 1)))

            with act.Fori(0, PAIRS - 1) as i:
                body(i, False)
            body(PAIRS - 1, True)

        @block.tensor
        def _(pe):
            def half(t, smp):
                return t[CC * smp:CC * smp + CC]

            pe.wait_ge(loaded, 16 * 5)
            pe.wait_ge(stats_done, 2 * PAIRS)
            nc.tensor.matmul(misc[0][:, 0:PAIRS], par("mean64"), moments[:, :, 0], start=True, stop=True)\
                .then_inc(gn_means, 1)
            pe.wait_ge(gn_offsets, 3)
            nc.tensor.matmul(misc[0][:, PAIRS:2 * PAIRS], par("mean64"), spread[:, :], start=True, stop=True)\
                .then_inc(gn_vars, 1)
            for smp in range(2):
                for hp in range(HP):
                    ins = nc.tensor.matmul(half(misc[1], smp)[:, 0:1], wo[:, hp, :], bv[:, hp:hp + 1],
                                           start=hp == 0, stop=hp == HP - 1)
            ins.then_inc(bias_product, 1)

            def project_qk(hp, n):
                cols = slice(hp * P, hp * P + P)
                for smp in range(2):
                    wait(pe, misc_free[smp], n[smp])
                for part, (w, src) in enumerate(((wq, xn), (wk, ct))):
                    for smp in range(2):
                        ins = nc.tensor.matmul(misc[smp][:, part * C:(part + 1) * C], half(w, smp)[:, cols],
                                               half(src, smp)[:, :], start=True, stop=True)
                        if part == 1:
                            ins.then_inc(misc_full[smp], 1)

            def project_v(hp, n):
                cols = slice(hp * P, hp * P + P)
                for smp in range(2):
                    wait(pe, misc_free[smp], n[smp])
                for k in range(QT):
                    for smp in range(2):
                        ins = nc.tensor.matmul(misc[smp][:, k * P:(k + 1) * P], half(ct, smp)[:, k * P:(k + 1) * P],
                                               half(wv, smp)[:, cols], start=True, stop=True)
                        if k == QT - 1:
                            ins.then_inc(misc_full[smp], 1)
                return ins

            def score(g, u):
                s, slot = u % 2, u % UNITS
                if not isinstance(g, int) or g > 0:
                    pe.wait_ge(probs_ready, 4 * (g - 1) + 1)
                for q in range(QT):
                    for h in range(2):
                        ins = nc.tensor.matmul(scores[s][h][:, q * C:(q + 1) * C],
                                               half(qk, h)[:, slot, 0, q * P:(q + 1) * P], half(qk, h)[:, slot, 1, :],
                                               start=True, stop=True)
                ins.then_inc(scores_ready, 1)

            def turn(g, u, h):
                s = u % 2
                pe.wait_ge(probs_ready, 4 * g + 2 * h + 3)
                pe.wait_ge(pT_ready, 2 * g + h + 1)
                for k in range(QT):
                    for q in range(QT):
                        ins = nc.tensor.transpose(turned[:, k * C + q * P:k * C + q * P + P],
                                                  probs[:, s, h, q, k * P:(k + 1) * P], ident)
                ins.then_inc(turned_ready, 1)

            def attend(g, u, h):
                pe.wait_ge(pT_ready, 2 * g + h + 2)
                if h == 0:
                    pe.wait_ge(y_ready, g + 1)
                for q in range(QT):
                    for k in range(QT):
                        ins = nc.tensor.matmul(attn[:, q, h, :], pT[:, h, k, q * P:(q + 1) * P], v[:, u, k, h, :],
                                               start=k == 0, stop=k == QT - 1)
                if h == 1:
                    ins.then_inc(attn_ready, 1)

            def turn_y(i, u, n):
                smp = u % 2
                pe.wait_ge(y_ready, UNITS * i + u + 2)
                wait(pe, misc_free[smp], n)
                for q in range(QT):
                    ins = nc.tensor.transpose(misc[smp][:, q * P:(q + 1) * P], y[:, smp, q, :], ident)
                ins.then_inc(misc_full[smp], 1)

            pe.wait_ge(bias_read, 1)
            pe.wait_ge(scaled_wq, 2)
            pe.wait_ge(xn_ready, 1)
            pe.wait_ge(ct_ready, 1)
            for hp in range(HP):
                project_qk(hp, [2 * hp] * 2)
                project_v(hp, [2 * hp + 1] * 2)
            for smp in range(2):
                pe.wait_ge(misc_free[smp], PROLOGUE)
            score(0, 0)

            def body(i, last):
                for u in range(UNITS):
                    g = UNITS * i + u
                    if not (last and u == UNITS - 1):
                        if u == UNITS - 1:
                            pe.wait_ge(misc_free[0], use(0, i, last, ("qk", 0)) + 1)
                        score(g + 1, u + 1)
                    turn(g, u, 0)
                    if u >= 1:
                        turn_y(i, u - 1, use((u - 1) % 2, i, last, ("yT", u - 1)))
                    if not last and u % 2 == 0 and u >= 2:
                        project_v(u // 2 - 1, [use(smp, i, last, ("v", u // 2 - 1)) for smp in range(2)])
                    attend(g, u, 0)
                    turn(g, u, 1)
                    if not last and u % 2 == 1:
                        if u == 1:
                            pe.wait_ge(xn_ready, i + 2)
                            pe.wait_ge(ct_ready, i + 2)
                        project_qk(u // 2, [use(smp, i, last, ("qk", u // 2)) for smp in range(2)])
                    attend(g, u, 1)
                if not last:
                    project_v(HP - 1, [use(smp, i, last, ("v", HP - 1)) for smp in range(2)])
                turn_y(i, UNITS - 1, use(1, i, last, ("yT", UNITS - 1)))
                n = use(0, i, last, ("out", 0))
                wait(pe, misc_free[0], n)
                pe.wait_ge(misc_free[1], use(1, i, last, ("yT", UNITS - 1)) + 1)
                for smp in range(2):
                    for hp in range(HP):
                        ins = nc.tensor.matmul(half(misc[0], smp)[:, 0:C], wo[:, hp, :], yT[:, smp, hp, :],
                                               start=hp == 0, stop=hp == HP - 1)
                ins.then_inc(misc_full[0], 1)

            with pe.Fori(0, PAIRS - 1) as i:
                body(i, False)
            body(PAIRS - 1, True)


@buffers
def layer1(nc, sb, sem, par, banks, X, shift_sb, state_sb, eps, out):
    ident, ones8, mean8 = par("ident"), par("ones8"), par("mean8")
    spread, gather = par("spread", HS, P), par("gather", HS, P)
    maa_w1, maa_w2, maa_w2g = par("maa_w1", CT, MAA * MD), par("maa_w2"), par("maa_w2g")
    decay_w1, decay_w2 = par("decay_w1", CT, DD), par("decay_w2")
    W = {n: par(n, CT, C) for n in SQUARES}
    vec = {n: par(n) for n in VECTORS}

    stat = sb("stat", [P, TT, 6])
    mom = sb("mom", [P, TT, 2])
    rstd = sb("rstd", [P, TT])
    xh = sb("xh", [P, TT, C])
    xa = sb("xa", [P, CT, G, L + 1])
    sx = sb("sx", [P, CT, GT])
    xx = sb("xx", [P, CT, GT])
    low1 = sb("low1", [P, GT])
    low2 = sb("low2", [MD, GT])
    xj = [sb(f"xj{j}", [P, CT, GT]) for j in range(MAA)]
    dh = sb("dh", [DD, GT])
    we = sb("we", [P, CT, GT])
    wd = sb("wd", [P, CT, G, L])
    r = sb("r", [P, CT, GT])
    k = sb("k", [P, CT, GT])
    v1 = sb("v1", [P, CT, GT])
    g = sb("g", [P, CT, GT])
    RING = 4
    a = sb("a", [P, RING, G, L])
    s = sb("s", [P, RING, GT])
    rs = sb("rs", [P, RING, GT])
    ruk = sb("ruk", [P, CT, GT])
    yc = sb("yc", [P, CT, GT])
    yd = sb("yd", [P, CT, GT])
    x2 = sb("x2", [P, TT, C])

    names = ["go", "col0", "st", "mo", "lg", "rs_", "xh", "xT", "xa", "sx", "xx", "low", "tanh", "mix", "mixt", "xj",
             "proj", "evac", "wdec", "sig", "gate", "vb", "a0", "a", "s", "rs", "y", "ruk", "q", "qv", "yc", "gm", "yd",
             "sq", "var", "lnv", "grs", "n1", "n2", "yg", "o", "x2", "fx", "fk", "fr", "kk", "kr", "kq", "rr", "rg",
             "f", "fm", "out", "stored", "group_free"]
    S = {n: sem("l1_" + n) for n in names}

    def grouped(t):
        return t.rearrange("p (b l) -> p b l", b=G)

    PROJ = [("dec1", 0), ("k", 0), ("k", 1), ("dec2", 0), ("dec2", 1), ("r", 0), ("r", 1), ("v", 0), ("v", 1),
            ("g", 0), ("g", 1)]
    NP = len(PROJ)
    NE = NP - 2
    MIX = [(j, c) for j in (0, 1, 3, 2, 4) for c in range(CT)]
    SRC = {"dec1": 0, "k": 1, "v": 2, "r": 3, "g": 4}
    STEPS = [(c, t) for c in range(CT) for t in range(HS)]
    NS = len(STEPS)

    with nc.Block() as block:
        @block.sync
        def _(sp):
            sp.sem_inc(S["group_free"], 1)
            with sp.Fori(0, GROUPS) as i:
                sp.wait_ge(S["out"], TT // 2 * (i + 1))
                sp.dma_start(out[:, bass.ds(i * TT, TT), :], xh[:, :, :]).then_inc(S["stored"], 16)
                sp.wait_ge(S["stored"], 16 * (i + 1))
                sp.sem_inc(S["group_free"], 1)

        @block.gpsimd
        def _(pool):
            ins = nc.gpsimd.memset(wd[:, :, :, 0:1], 0.0)
            with pool.Fori(0, GROUPS) as i:
                def col0(which, n):
                    for c in range(CT):
                        ins = nc.gpsimd.tensor_copy(xa[:, c, :, 0], shift_sb[:, which, c, bass.ds(i * G, G)])
                        ins.then_inc(S["col0"], 1)

                def diff(n):
                    for c in range(CT):
                        pool.wait_ge(S["xa"], 2 * CT * i + n * CT + c + 1)
                        if c == 0:
                            pool.wait_ge(S["col0"], 2 * CT * i + (n + 1) * CT)
                        nc.gpsimd.tensor_tensor(grouped(sx[:, c, :]), xa[:, c, :, 0:L], xa[:, c, :, 1:L + 1],
                                                ALU.subtract).then_inc(S["sx"], 1)

                pool.wait_ge(S["group_free"], i + 1)
                col0(1, 0)
                diff(0)
                for n, (j, c) in enumerate(MIX):
                    pool.wait_ge(S["mixt"], len(MIX) * i + n + 1)
                    nc.gpsimd.tensor_tensor(grouped(xj[j][:, c, :]), grouped(xj[j][:, c, :]), xa[:, c, :, 1:L + 1],
                                            ALU.add).then_inc(S["xj"], 1)
                for n, (c, t) in enumerate(STEPS):
                    if n < RING:
                        nc.gpsimd.tensor_copy(a[:, n % RING, :, 0], state_sb[:, c, t, bass.ds(i * G, G)])\
                            .then_inc(S["a0"], 1)
                if True:
                    for n, (c, t) in enumerate(STEPS):
                        m = n % RING
                        pool.wait_ge(S["s"], NS * i + n + 1)
                        if n + RING < NS:
                            cn, tn = STEPS[n + RING]
                            nc.gpsimd.tensor_copy(a[:, m, :, 0], state_sb[:, cn, tn, bass.ds(i * G, G)])\
                                .then_inc(S["a0"], 1)
                        pool.wait_ge(S["evac"], NE * i + 7)
                        if n >= RING:
                            pool.wait_ge(S["y"], NS * i + (n - RING + 1))
                        nc.gpsimd.tensor_tensor(rs[:, m, :], r[:, c, :], s[:, m, :], ALU.mult).then_inc(S["rs"], 1)
                pool.wait_ge(S["x2"], 2 * (i + 1))
                col0(0, 1)
                diff(1)
                for c in range(CT):
                    pool.wait_ge(S["kr"], CT * i + c + 1)
                    nc.gpsimd.tensor_tensor(xj[2][:, c, :], we[:, c, :], we[:, c, :], ALU.mult).then_inc(S["kq"], 1)
                for b in range(2):
                    pool.wait_ge(S["fm"], 2 * i + b + 1)
                    nc.gpsimd.tensor_tensor(xh[:, 2 * b:2 * b + 2, :], yd[:, b, :].rearrange("p (a n) -> p a n", a=2),
                                            x2[:, 2 * b:2 * b + 2, :], ALU.add).then_inc(S["out"], 1)

        @block.vector
        def _(dve):
            with dve.Fori(0, GROUPS) as i:
                dve.wait_ge(S["group_free"], i + 1)

                def layernorm(n, tile):
                    for j in range(TT):
                        nc.vector.bn_stats(stat[:, j, :], tile(j)).then_inc(S["st"], 1)
                    dve.wait_ge(S["st"], 2 * TT * i + (n + 1) * TT)
                    dve.sem_inc(S["go"], 1)
                    for j in range(TT):
                        nc.vector.bn_aggr(mom[:, j, :], stat[:, j, :]).then_inc(S["mo"], 1)
                    dve.wait_ge(S["rs_"], 2 * i + n + 1)
                    for j in range(TT):
                        nc.vector.tensor_scalar(xh[:, j, :], tile(j), mom[:, j, 0:1], rstd[:, j:j + 1],
                                                ALU.subtract, ALU.mult).then_inc(S["xh"], 1)

                layernorm(0, lambda j: X[:, bass.ds(i * TT + j, 1), :].rearrange("p a n -> p (a n)"))
                for c in range(CT):
                    dve.wait_ge(S["sx"], 2 * CT * i + c + 1)
                    nc.vector.scalar_tensor_tensor(grouped(xx[:, c, :]), grouped(sx[:, c, :]),
                                                   vec["maa_x"][:, c:c + 1], xa[:, c, :, 1:L + 1],
                                                   ALU.mult, ALU.add).then_inc(S["xx"], 1)
                maa = ["maa_w", "maa_k", "maa_v", "maa_r", "maa_g"]
                for n, (j, c) in enumerate(MIX):
                    dve.wait_ge(S["mix"], len(MIX) * i + n + 1)
                    nc.vector.scalar_tensor_tensor(xj[j][:, c, :], banks[4 + n % 4][:, :], vec[maa[j]][:, c:c + 1],
                                                   sx[:, c, :], ALU.add, ALU.mult).then_inc(S["mixt"], 1)
                for c in range(CT):
                    dve.wait_ge(S["evac"], NE * i + 6 + c)
                    nc.vector.scalar_tensor_tensor(ruk[:, c, :], k[:, c, :], vec["faaaa"][:, c:c + 1], r[:, c, :],
                                                   ALU.mult, ALU.mult).then_inc(S["ruk"], 1)
                def gates():
                    for c in range(CT):
                        dve.wait_ge(S["sig"], CT * i + c + 1)
                        nc.vector.tensor_tensor(g[:, c, :], banks[(9 + c) % 4][:, :], g[:, c, :], ALU.mult)\
                            .then_inc(S["gate"], 1)
                gates()
                dve.wait_ge(S["wdec"], CT * (i + 1))
                for n, (c, t) in enumerate(STEPS):
                    m = n % RING
                    dve.wait_ge(S["vb"], NS * i + n + 1)
                    nc.vector.tensor_tensor(a[:, m, :, 1:L], grouped(banks[4 + m][:, :])[:, :, 0:L - 1],
                                            grouped(k[:, c, :])[:, :, 0:L - 1], ALU.mult).then_inc(S["a"], 1)
                    dve.wait_ge(S["a"], NS * i + n + 1)
                    dve.wait_ge(S["a0"], NS * i + n + 1)
                    if n >= RING:
                        dve.wait_ge(S["rs"], NS * i + (n - RING + 1))
                    nc.vector.tensor_tensor_scan(s[:, m, :], wd[:, c, :, :].rearrange("p b l -> p (b l)"),
                                                 a[:, m, :, :].rearrange("p b l -> p (b l)"), 0.0,
                                                 ALU.mult, ALU.add).then_inc(S["s"], 1)
                for c in range(CT):
                    dve.wait_ge(S["q"], CT * i + c + 1)
                    nc.vector.tensor_tensor(yd[:, c, :], banks[2 + c][:, :], v1[:, c, :], ALU.mult).then_inc(S["qv"], 1)
                for c in range(CT):
                    dve.wait_ge(S["qv"], CT * i + c + 1)
                    dve.wait_ge(S["y"], NS * i + (c + 1) * HS)
                    nc.vector.tensor_tensor(yc[:, c, :], banks[c][:, :], yd[:, c, :], ALU.add).then_inc(S["yc"], 1)
                for c in range(CT):
                    dve.wait_ge(S["gm"], CT * i + c + 1)
                    nc.vector.tensor_tensor(yd[:, c, :], yc[:, c, :], banks[2 + c][:, :], ALU.subtract)\
                        .then_inc(S["yd"], 1)
                for c in range(CT):
                    dve.wait_ge(S["grs"], CT * i + c + 1)
                    nc.vector.tensor_tensor(yd[:, c, :], yd[:, c, :], yc[:, c, :], ALU.mult).then_inc(S["n1"], 1)
                for c in range(CT):
                    dve.wait_ge(S["n1"], CT * i + c + 1)
                    nc.vector.tensor_scalar(yd[:, c, :], yd[:, c, :], vec["gn_w"][:, c:c + 1], vec["gn_b"][:, c:c + 1],
                                            ALU.mult, ALU.add).then_inc(S["n2"], 1)
                for c in range(CT):
                    dve.wait_ge(S["n2"], CT * i + c + 1)
                    nc.vector.tensor_tensor(yc[:, c, :], yd[:, c, :], g[:, c, :], ALU.mult).then_inc(S["yg"], 1)
                for b in range(2):
                    dve.wait_ge(S["o"], 2 * i + b + 1)
                    nc.vector.tensor_tensor(x2[:, 2 * b:2 * b + 2, :], banks[4 + b][:, :].rearrange("p (a n) -> p a n", a=2),
                                            X[:, bass.ds(i * TT + 2 * b, 2), :], ALU.add).then_inc(S["x2"], 1)
                dve.wait_ge(S["x2"], 2 * (i + 1))
                layernorm(1, lambda j: x2[:, j, :])
                for c in range(CT):
                    dve.wait_ge(S["sx"], 2 * CT * i + CT + c + 1)
                    for which, (name, done) in enumerate((("fmaa_k", "fk"), ("fmaa_r", "fr"))):
                        nc.vector.scalar_tensor_tensor(grouped(xj[which][:, c, :]), grouped(sx[:, c, :]),
                                                       vec[name][:, c:c + 1], xa[:, c, :, 1:L + 1],
                                                       ALU.mult, ALU.add).then_inc(S[done], 1)
                for b in range(2):
                    dve.wait_ge(S["f"], 2 * i + b + 1)
                    dve.wait_ge(S["rg"], 2 * i + b + 1)
                    nc.vector.tensor_tensor(yd[:, b, :], banks[4 + b][:, :], yc[:, b, :], ALU.mult)\
                        .then_inc(S["fm"], 1)

        @block.scalar
        def _(act):
            with act.Fori(0, GROUPS) as i:
                act.wait_ge(S["group_free"], i + 1)

                def rstds(n):
                    act.wait_ge(S["mo"], 2 * TT * i + (n + 1) * TT)
                    nc.scalar.activation(rstd[:, :], mom[:, :, 1], ACT.Ln, bias=eps[:, 0:1]).then_inc(S["lg"], 1)
                    act.wait_ge(S["lg"], 2 * i + n + 1)
                    nc.scalar.activation(rstd[:, :], rstd[:, :], ACT.Exp, scale=-0.5).then_inc(S["rs_"], 1)

                def affine(n, w, b, bank):
                    for c in range(CT):
                        act.wait_ge(S["xT"], 2 * CT * i + n * CT + c + 1)
                        nc.scalar.activation(xa[:, c, :, 1:L + 1], grouped(banks[bank + c][:, :]), ACT.Identity,
                                             scale=vec[w][:, c:c + 1], bias=vec[b][:, c:c + 1]).then_inc(S["xa"], 1)

                rstds(0)
                affine(0, "ln1_w", "ln1_b", 0)
                act.wait_ge(S["low"], 2 * i + 1)
                nc.scalar.activation(low1[:, :], banks[2][:, :], ACT.Tanh).then_inc(S["tanh"], 1)
                act.wait_ge(S["low"], 2 * i + 2)
                nc.scalar.activation(low2[:, :], banks[3][0:MD, :], ACT.Tanh).then_inc(S["tanh"], 1)
                dst = {"k": k, "r": r, "v": v1}
                for n, (name, c) in enumerate(PROJ):
                    act.wait_ge(S["proj"], NP * i + n + 1)
                    bank = banks[n % 4]
                    if name == "dec1":
                        nc.scalar.activation(dh[:, :], bank[0:DD, :], ACT.Tanh).then_inc(S["evac"], 1)
                    elif name == "dec2":
                        nc.scalar.activation(we[:, c, :], bank[:, :], ACT.Exp, bias=vec["time_decay"][:, c:c + 1])\
                            .then_inc(S["evac"], 1)
                        act.wait_ge(S["evac"], NE * i + n + 1)
                        nc.scalar.activation(wd[:, c, :, 1:L], grouped(we[:, c, :])[:, :, 0:L - 1], ACT.Exp, scale=-1.0)\
                            .then_inc(S["wdec"], 1)
                    elif name == "g":
                        nc.scalar.activation(g[:, c, :], bank[:, :], ACT.Sigmoid).then_inc(S["sig"], 1)
                    else:
                        nc.scalar.copy(dst[name][:, c, :], bank[:, :]).then_inc(S["evac"], 1)
                for c in range(CT):
                    act.wait_ge(S["yd"], CT * i + c + 1)
                    nc.scalar.activation(xx[:, c, :], yd[:, c, :], ACT.Square).then_inc(S["sq"], 1)
                for c in range(CT):
                    act.wait_ge(S["var"], CT * i + c + 1)
                    nc.scalar.activation(xx[:, c, :], banks[c][:, :], ACT.Ln, bias=eps[:, 0:1]).then_inc(S["lnv"], 1)
                for c in range(CT):
                    act.wait_ge(S["lnv"], CT * i + c + 1)
                    nc.scalar.activation(yc[:, c, :], xx[:, c, :], ACT.Exp, scale=-0.5).then_inc(S["grs"], 1)
                rstds(1)
                affine(1, "ln2_w", "ln2_b", 6)
                for c in range(CT):
                    act.wait_ge(S["kk"], CT * i + c + 1)
                    nc.scalar.activation(we[:, c, :], banks[c][:, :], ACT.Relu).then_inc(S["kr"], 1)
                for b in range(2):
                    act.wait_ge(S["rr"], 2 * i + b + 1)
                    nc.scalar.activation(yc[:, b, :], banks[2 + b][:, :], ACT.Sigmoid).then_inc(S["rg"], 1)

        @block.tensor
        def _(pe):
            with pe.Fori(0, GROUPS) as i:
                pe.wait_ge(S["group_free"], i + 1)

                def turn(n, bank):
                    for c in range(CT):
                        for j in range(TT):
                            if c == 0:
                                pe.wait_ge(S["xh"], 2 * TT * i + n * TT + j + 1)
                            ins = nc.tensor.transpose(banks[bank + c][:, j * P:(j + 1) * P], xh[:, j, c * P:(c + 1) * P],
                                                      ident)
                        ins.then_inc(S["xT"], 1)

                def product(bank, w, src, co):
                    for ci in range(CT):
                        ins = nc.tensor.matmul(bank, w[:, ci, co], src[:, ci, :], start=ci == 0, stop=ci == CT - 1)
                    return ins

                def token_product(b, w, src, bank):
                    for j in range(2):
                        tok = slice((2 * b + j) * P, (2 * b + j + 1) * P)
                        for ci in range(CT):
                            ins = nc.tensor.matmul(banks[bank + b][:, j * C:(j + 1) * C], src[:, ci, tok], w[:, ci, :],
                                                   start=ci == 0, stop=ci == CT - 1)
                    return ins

                turn(0, 0)
                pe.wait_ge(S["xx"], CT * (i + 1))
                product(banks[2][:, :], maa_w1, xx, slice(0, P)).then_inc(S["low"], 1)
                product(banks[3][0:MD, :], maa_w1, xx, slice(P, P + MD)).then_inc(S["low"], 1)
                for n, (j, c) in enumerate(MIX):
                    pe.wait_ge(S["tanh"], 2 * i + (2 if j == 4 else 1))
                    if n >= 4:
                        pe.wait_ge(S["mixt"], len(MIX) * i + (n - 3))
                    w, src, at = (maa_w2g, low2, 0) if j == 4 else (maa_w2, low1, MD * j)
                    nc.tensor.matmul(banks[4 + n % 4][:, :], w[at:at + MD, c * P:(c + 1) * P], src[at:at + MD, :],
                                     start=True, stop=True).then_inc(S["mix"], 1)
                order = [j for j, c in MIX if c == 1]
                for n, (name, c) in enumerate(PROJ):
                    if n >= 4:
                        pe.wait_ge(S["evac"], NE * i + (n - 3))
                    if n == 0:
                        pe.wait_ge(S["tanh"], 2 * (i + 1))
                    bank = banks[n % 4]
                    if name == "dec2":
                        pe.wait_ge(S["evac"], NE * i + 1)
                        ins = nc.tensor.matmul(bank[:, :], decay_w2[0:DD, c * P:(c + 1) * P], dh[:, :],
                                               start=True, stop=True)
                    else:
                        j = SRC[name]
                        pe.wait_ge(S["xj"], len(MIX) * i + CT * (order.index(j) + 1))
                        if name == "dec1":
                            ins = product(bank[0:DD, :], decay_w1, xj[j], slice(0, DD))
                        else:
                            ins = product(bank[:, :], W["W" + name], xj[j], slice(c * P, (c + 1) * P))
                    ins.then_inc(S["proj"], 1)

                pe.wait_ge(S["mixt"], len(MIX) * (i + 1))
                pe.wait_ge(S["evac"], NE * (i + 1))

                def spread_v(n):
                    c, t = STEPS[n]
                    if n >= RING:
                        pe.wait_ge(S["a"], NS * i + (n - RING + 1))
                    nc.tensor.matmul(banks[4 + n % RING][:, :], spread[:, t, :], v1[:, c, :], start=True, stop=True)\
                        .then_inc(S["vb"], 1)

                def sum_rs(n):
                    c, t = STEPS[n]
                    pe.wait_ge(S["rs"], NS * i + n + 1)
                    nc.tensor.matmul(banks[c][:, :], gather[:, t, :], rs[:, n % RING, :], start=t == 0,
                                     stop=t == HS - 1).then_inc(S["y"], 1)

                for n in range(RING):
                    spread_v(n)
                pe.wait_ge(S["gate"], CT * (i + 1))
                for c in range(CT):
                    pe.wait_ge(S["ruk"], CT * i + c + 1)
                    nc.tensor.matmul(banks[2 + c][:, :], ones8, ruk[:, c, :], start=True, stop=True).then_inc(S["q"], 1)
                for n in range(NS):
                    if n + RING < NS:
                        spread_v(n + RING)
                    sum_rs(n)
                for c in range(CT):
                    pe.wait_ge(S["yc"], CT * i + c + 1)
                    nc.tensor.matmul(banks[2 + c][:, :], mean8, yc[:, c, :], start=True, stop=True).then_inc(S["gm"], 1)
                for c in range(CT):
                    pe.wait_ge(S["sq"], CT * i + c + 1)
                    nc.tensor.matmul(banks[c][:, :], mean8, xx[:, c, :], start=True, stop=True).then_inc(S["var"], 1)
                pe.wait_ge(S["yg"], CT * (i + 1))
                for b in range(2):
                    token_product(b, W["Wo"], yc, 4).then_inc(S["o"], 1)
                turn(1, 6)
                pe.wait_ge(S["fk"], CT * (i + 1))
                for c in range(CT):
                    product(banks[c][:, :], W["fWk"], xj[0], slice(c * P, (c + 1) * P)).then_inc(S["kk"], 1)
                pe.wait_ge(S["fr"], CT * (i + 1))
                for b in range(2):
                    token_product(b, W["fWr"], xj[1], 2).then_inc(S["rr"], 1)
                pe.wait_ge(S["kq"], CT * (i + 1))
                for b in range(2):
                    token_product(b, W["fWv"], xj[2], 4).then_inc(S["f"], 1)


def constants():
    p = np.arange(P)
    head = p[:, None] // HS == p[None, :] // HS
    sample = (p[:, None] // CC == p[None, :] // CC).astype(np.float32)
    spread = np.stack([(head & (p[:, None] % HS == t)) for t in range(HS)], 1).astype(np.float32)
    gather = np.stack([(head & (p[None, :] % HS == t)) for t in range(HS)], 1).astype(np.float32)
    head = head.astype(np.float32)
    return {"ident": np.eye(P, dtype=np.float32), "mean64": sample / np.float32(CC), "ones8": head,
            "mean8": head / np.float32(HS), "spread": spread.reshape(P, -1), "gather": gather.reshape(P, -1)}


def pack(inputs):
    def l0(name):
        return np.asarray(inputs["L0_xattn_" + name])

    def l1(name):
        return np.asarray(inputs["L1_xattn_" + name])

    def twice(a):
        return np.concatenate([a, a], 0)

    def tiles(a):
        return a.reshape(-1, P, a.shape[1]).transpose(1, 0, 2).reshape(P, -1)

    def padded(a):
        full = np.zeros((P, a.shape[1]), a.dtype)
        full[:a.shape[0]] = a
        return full

    kw, vw = l0("Wkv")[:HP * P], l0("Wkv")[HP * P:]
    f = {"wq": twice(l0("Wq").T), "wk": twice(kw.T), "wv": twice(vw.T), "wo": tiles(l0("Wo").T),
         "bq": l0("bq").reshape(HP, P).T, "bk": l0("bkv")[:HP * P].reshape(HP, P).T,
         "bv": l0("bkv")[HP * P:].reshape(HP, P).T,
         "gamma": twice(l0("gamma")[:, None]), "beta": twice(l0("beta")[:, None]), "bo": twice(l0("bo")[:, None]),
         "maa_w1": tiles(l1("maa_w1")), "maa_w2": l1("maa_w2")[:4].reshape(P, C), "maa_w2g": padded(l1("maa_w2")[4]),
         "decay_w1": tiles(l1("decay_w1")), "decay_w2": padded(l1("decay_w2")), **constants()}
    for name in VECTORS:
        f[name] = l1(name).reshape(CT, P).T
    for name in SQUARES:
        f[name] = tiles(l1(name).T)
    return np.ascontiguousarray(np.concatenate([f[name] for name, _ in FIELDS], 1))


def kernel(**inputs):
    import concourse.bacc as bacc
    from concourse.bass_utils import run_bass_kernel_spmd

    x = np.ascontiguousarray(np.asarray(inputs["x"]).reshape(PAIRS, P, C))
    context = np.asarray(inputs["ctx_2048"])
    ctx = np.ascontiguousarray(context.reshape(PAIRS, P, C))
    shift = np.ascontiguousarray(context[:, 0:2].reshape(B, 2, CT, P).transpose(3, 1, 2, 0))
    state = np.ascontiguousarray(context[:, 2:2 + HS].reshape(B, CT, P, HS).transpose(2, 1, 3, 0))
    arrays = {"x_dram": x, "ctx_dram": ctx, "params_dram": pack(inputs), "shift_dram": shift, "state_dram": state}

    nc = bacc.Bacc("TRN2", target_bir_lowering=False, num_devices=1)
    aps = {n: nc.dram_tensor(n, v.shape, FP32, kind="ExternalInput").ap() for n, v in arrays.items()}
    out = nc.dram_tensor("out_dram", (PAIRS, P, C), FP32, kind="ExternalOutput").ap()
    build(nc, aps["x_dram"].rearrange("a p n -> p a n"), aps["ctx_dram"].rearrange("a p n -> p a n"),
          aps["params_dram"], aps["shift_dram"], aps["state_dram"], out.rearrange("a p n -> p a n"))
    result = run_bass_kernel_spmd(nc, [arrays], core_ids=[0])
    return np.asarray(result.results[0]["out_dram"]).reshape(B, L, C)
```

```python
import numpy as np
import concourse.bass as bass
from concourse import mybir
from concourse.alu_op_type import AluOpType as ALU
from contextlib import ExitStack

FP32 = mybir.dt.float32
FR = mybir.dt.float32r
ACT = mybir.ActivationFunctionType

B, L, C = 32, 64, 256
P = 128
PAIRS = B // 2
CC = 64
HP = 4
UNITS = 2 * HP
QT = C // P
VW = CC + 1
G = 8
GROUPS = B // G
GT = G * L
TT = GT // P
CT = C // P
HS = 8
MAA = 5
MD = 32
DD = 64
EPS = 1e-5

VECTORS = ["ln1_w", "ln1_b", "ln2_w", "ln2_b", "maa_x", "maa_w", "maa_k", "maa_v", "maa_r", "maa_g",
           "time_decay", "faaaa", "gn_w", "gn_b", "fmaa_k", "fmaa_r"]
SQUARES = ["Wr", "Wk", "Wv", "Wg", "Wo", "fWk", "fWr", "fWv"]

FIELDS0 = [("wqn", HP * P), ("wkn", HP * P), ("wvn", HP * P), ("bqz", HP * P), ("wo", HP * CC), ("bv", HP),
           ("gamma", 1), ("beta", 1), ("bo", 1), ("is_hi", 1), ("is_lo", 1), ("mean64", P), ("pick", 2 * P)]
FIELDS = [*[(n, CT) for n in VECTORS],
          ("maa_w1", CT * MAA * MD), ("maa_w2", C), ("maa_w2g", C), ("decay_w1", CT * DD), ("decay_w2", C),
          *[(n, CT * C) for n in SQUARES],
          ("ident", P), ("ones8", P), ("mean8", P), ("spread", HS * P), ("gather", HS * P)]


def offsets(fields):
    at, out = 0, {}
    for name, width in fields:
        out[name] = (at, width)
        at += width
    return out, at


OFF, WIDTH = offsets(FIELDS)
OFF0, WIDTH0 = offsets(FIELDS0)


def build(nc, x, xs, ctxs, params, params0, shift, state, out):
    es = ExitStack()
    with es:
        def sb(name, shape):
            return es.enter_context(nc.sbuf_tensor(name, shape, FP32))

        def sem(name):
            return es.enter_context(nc.semaphore(name))

        params_sb = sb("params_sb", [P, WIDTH])

        def par(name, *dims):
            at, width = OFF[name]
            v = params_sb[:, at:at + width]
            if len(dims) == 2:
                v = v.rearrange("p (a b) -> p a b", a=dims[0])
            return v

        banks = [es.enter_context(nc.psum_tensor(f"bank{b}", [P, 512], FP32)) for b in range(8)]

        X = sb("X", [P, PAIRS, C])
        shift_sb = sb("shift_sb", [P, 2, CT, B])
        state_sb = sb("state_sb", [P, CT, HS, B])
        eps = sb("eps", [P, 1])

        layer0(nc, sem, par("ident"), banks, X, shift_sb, state_sb, eps, params_sb, x, xs, ctxs, params, params0,
               shift, state)
        layer1(nc, sem, par, banks, X, shift_sb, state_sb, eps, out)


def buffers(build_layer):
    def run(nc, *args):
        with ExitStack() as es:
            build_layer(nc, lambda name, shape, dtype=FP32: es.enter_context(nc.sbuf_tensor(name, shape, dtype)),
                        *args)
    return run


@buffers
def layer0(nc, sb, sem, ident, banks, X, shift_sb, state_sb, eps, params_sb, x, xs, ctxs, params, params0, shift,
           state):
    p0 = sb("params0_sb", [P, WIDTH0])

    def par0(name, *dims):
        at, width = OFF0[name]
        t = p0[:, at:at + width]
        return t.rearrange("p (a b) -> p a b", a=dims[0]) if dims else t

    wqn, wkn, wvn, bqz = (par0(n, HP, P) for n in ("wqn", "wkn", "wvn", "bqz"))
    wo = par0("wo", HP, CC)
    bv, pick = par0("bv"), par0("pick", 2, P)
    is_hi, is_lo = par0("is_hi"), par0("is_lo")
    H = 2 * HP

    stats = sb("stats", [P, PAIRS, 6])
    moments = sb("moments", [P, PAIRS, 2])
    offset = sb("offset", [P, PAIRS])
    spread = sb("spread_sq", [P, PAIRS])
    rstd = sb("gn_rstd_sb", [P, B])
    gn_scale = sb("gn_scale", [P, B])
    gn_shift = sb("gn_shift", [P, B])
    shift_neg = sb("shift_neg", [P, B])
    out_bias = sb("out_bias", [P, 1])
    wtmp = sb("wtmp", [P, H, P])
    btmp = sb("btmp", [P, H, P])
    bres = sb("bres", [P, H, P])
    bhi = sb("bhi", [P, H, P], FR)
    w1 = sb("w1", [P, H, P], FR)
    w2 = sb("w2", [P, H, P], FR)
    wz = sb("wz", [P, H, CC], FR)
    xd = [sb(f"xd{s}", [P, C]) for s in range(2)]
    cd = [sb(f"cd{s}", [P, C]) for s in range(2)]
    xn = sb("xn", [P, C])
    x1 = [sb(f"x1_{s}", [P, C], FR) for s in range(2)]
    x2 = [sb(f"x2_{s}", [P, C], FR) for s in range(2)]
    c1 = [sb(f"c1_{s}", [P, C], FR) for s in range(2)]
    c2 = [sb(f"c2_{s}", [P, C], FR) for s in range(2)]
    qq = sb("qq", [P, 4, 2, C], FR)
    z = [sb(f"z{s}", [P, QT, H * CC]) for s in range(2)]
    probs = sb("probs", [P, 2, 2, QT, C])
    neg_max = sb("neg_max", [P, 2, 4])
    sums = sb("sums", [P, 2, 4])
    recip = sb("recip", [P, 2, 4])
    pT = sb("pT", [P, 2, QT, C])
    o = sb("o", [P, QT, P])

    scores = [[banks[0], banks[1]], [banks[2], banks[3]]]
    turned = banks[4]
    acc = [banks[5][:, s * P:(s + 1) * P].rearrange("p (q c) -> p q c", q=QT) for s in range(2)]
    out_T = banks[5][:, 2 * P:4 * P]
    misc = [banks[6], banks[7]]

    def z_half(parity):
        return banks[4 + parity][:, 0:HP * CC].rearrange("p (h c) -> p h c", h=HP)

    loaded = sem("loaded")
    loaded_params = sem("loaded_params")
    state_loaded = sem("state_loaded")
    sample_loaded = [sem("sample_loaded0"), sem("sample_loaded1")]
    stats_done = sem("stats_done")
    gn_means = sem("gn_means")
    gn_offsets = sem("gn_offsets")
    gn_vars = sem("gn_vars")
    gn_log = sem("gn_log")
    gn_rstd = sem("gn_rstd")
    gn_affine = sem("gn_affine")
    eps_set = sem("eps_set")
    ones_set = sem("ones_set")
    folded = sem("folded")
    split = sem("split")
    weights_ready = sem("weights_ready")
    xn_ready = sem("xn_ready")
    rounded = sem("rounded")
    prepared = sem("prepared")
    x_hi = sem("x_hi")
    x_parts = sem("x_parts")
    scores_ready = sem("scores_ready")
    max_ready = sem("max_ready")
    probs_ready = sem("probs_ready")
    recip_ready = sem("recip_ready")
    norm_ready = sem("norm_ready")
    turned_ready = sem("turned_ready")
    pT_ready = sem("pT_ready")
    pool_went = sem("pool_went")
    qq_full = sem("qq_full")
    qq_hi = sem("qq_hi")
    qq_ready = sem("qq_ready")
    z_full = sem("z_full")
    z_ready = sem("z_ready")
    acc_ready = sem("acc_ready")
    o_ready = sem("o_ready")
    out_ready = sem("out_ready")

    ITEMS = {0: [("qq", 0)], 1: [("qq", 1), ("z", 0)], 2: [("qq", 2), ("z", 1)], 3: [("qq", 3)]}
    TURN = {("qq", 0): 0, ("qq", 1): 1, ("z", 0): 2, ("qq", 2): 3, ("z", 1): 4, ("qq", 3): 5}

    def bank_of(item):
        return misc[TURN[item] % 2]

    U = HP
    LAST = U * B

    with nc.Block() as block:
        @block.sync
        def _(sp):
            for q in range(4):
                sl = slice(q * PAIRS // 4, (q + 1) * PAIRS // 4)
                sp.dma_start(X[:, sl, :], x[:, sl, :]).then_inc(loaded, 16)

            def load(n, par):
                for half in range(2):
                    rows = slice(CC * half, CC * half + CC)
                    sp.dma_start(xd[par][rows, :], xs[bass.ds(n, 1), :, :]).then_inc(sample_loaded[par], 16)
                    sp.dma_start(cd[par][rows, :], ctxs[bass.ds(n, 1), :, :]).then_inc(sample_loaded[par], 16)

            load(0, 0)
            load(1, 1)
            sp.dma_start(shift_sb[:, :, :, :], shift).then_inc(state_loaded, 16)
            sp.dma_start(state_sb[:, :, :, :], state).then_inc(state_loaded, 16)
            with sp.Fori(0, PAIRS - 1) as i:
                for par in range(2):
                    sp.wait_ge(prepared, 2 * i + (par + 1))
                    sp.wait_ge(xn_ready, 2 * i + (par + 1))
                    load(2 * i + par + 2, par)
            sp.wait_ge(state_loaded, 32)

        @block.gpsimd
        def _(pool):
            def wait_apart(semaphore, value):
                pool.wait_ge(semaphore, value)
                pool.sem_inc(pool_went, 1)

            def prepare(n, par, loads):
                wait_apart(sample_loaded[par], 64 * loads)
                nc.gpsimd.tensor_scalar(c1[par][:, :], cd[par][:, :], 1.0, 0.0, ALU.mult, ALU.add)\
                    .then_inc(rounded, 1)
                pool.wait_ge(rounded, n + 1)
                nc.gpsimd.tensor_tensor(c2[par][:, :], cd[par][:, :], c1[par][:, :].bitcast(FP32), ALU.subtract)\
                    .then_inc(prepared, 1)
                wait_apart(xn_ready, n + 1)
                nc.gpsimd.tensor_scalar(x1[par][:, :], xn[:, :], 1.0, 0.0, ALU.mult, ALU.add).then_inc(x_hi, 1)

            def normalise(g, u):
                s = u % 2
                wait_apart(recip_ready, g + 1)
                for h in range(2):
                    for q in range(QT):
                        n = 2 * h + q
                        row = probs[:, s, h, q, :]
                        nc.gpsimd.tensor_scalar(row, row, recip[:, s, n:n + 1], 1.0, ALU.mult, ALU.mult)\
                            .then_inc(norm_ready, 1)

            prepare(0, 0, 1)
            prepare(1, 1, 1)
            normalise(0, 0)

            def body(i, last):
                for s in range(2):
                    for v in range(U):
                        g = 2 * U * i + (U * s + v)
                        if not last or U * s + v + 1 < 2 * U:
                            normalise(g + 1, v + 1)
                        if v == 2 and not last:
                            prepare(2 * i + (s + 2), s, i + 2)

            with pool.Fori(0, PAIRS - 1) as i:
                body(i, False)
            body(PAIRS - 1, True)

        @block.vector
        def _(dve):
            def shape3(bank):
                return bank[:, :].rearrange("p (a n) -> p a n", a=2)

            dve.sem_inc(pT_ready, 1)
            nc.vector.memset(eps[:, :], EPS).then_inc(eps_set, 1)
            for s in range(2):
                nc.vector.memset(x2[s][CC:P, :].bitcast(FP32), 0.0).then_inc(ones_set, 1)
                dve.wait_ge(ones_set, 2 * s + 1)
                nc.vector.memset(x2[s][CC:CC + 2, :].bitcast(FP32), 1.0).then_inc(ones_set, 1)
            dve.wait_ge(loaded, 16 * 4)
            for p in range(PAIRS):
                nc.vector.bn_stats(stats[:, p, :], X[:, p, :]).then_inc(stats_done, 1)
            for p in range(PAIRS):
                dve.wait_ge(stats_done, p + 1)
                nc.vector.bn_aggr(moments[:, p, :], stats[:, p, :]).then_inc(stats_done, 1)
            mean, var = moments[:, :, 0], moments[:, :, 1]
            dve.wait_ge(stats_done, 2 * PAIRS)
            dve.wait_ge(gn_means, 1)
            nc.vector.tensor_tensor(offset[:, :], mean, misc[0][:, 0:PAIRS], ALU.subtract).then_inc(gn_offsets, 1)
            dve.wait_ge(gn_offsets, 1)
            nc.vector.tensor_tensor(spread[:, :], offset[:, :], offset[:, :], ALU.mult).then_inc(gn_offsets, 1)
            dve.wait_ge(gn_offsets, 2)
            nc.vector.tensor_tensor(spread[:, :], spread[:, :], var, ALU.add).then_inc(gn_offsets, 1)
            dve.wait_ge(gn_rstd, 1)
            nc.vector.tensor_scalar(gn_scale[:, :], rstd[:, :], par0("gamma"), None, ALU.mult).then_inc(gn_affine, 1)
            dve.wait_ge(gn_affine, 1)
            nc.vector.tensor_tensor(shift_neg[:, :], gn_scale[:, :], misc[0][:, B:2 * B], ALU.mult)\
                .then_inc(gn_affine, 1)
            dve.wait_ge(gn_affine, 2)
            nc.vector.tensor_scalar(gn_shift[:, :], shift_neg[:, :], -1.0, par0("beta"), ALU.mult, ALU.add)\
                .then_inc(gn_affine, 1)
            dve.wait_ge(gn_affine, 3)

            def affine(n, par, loads):
                dve.wait_ge(sample_loaded[par], 64 * loads)
                nc.vector.tensor_scalar(xn[:, :], xd[par][:, :], gn_scale[:, bass.ds(n, 1)],
                                        gn_shift[:, bass.ds(n, 1)], ALU.mult, ALU.add).then_inc(xn_ready, 1)

            def lower_part(n, par):
                dve.wait_ge(x_hi, n + 1)
                nc.vector.tensor_tensor(x2[par][0:CC, :], xn[0:CC, :], x1[par][0:CC, :].bitcast(FP32), ALU.subtract)\
                    .then_inc(x_parts, 1)
                dve.wait_ge(x_parts, n + 1)

            affine(0, 0, 1)
            dve.wait_ge(folded, 1)
            for b in range(2):
                nc.vector.tensor_scalar(wtmp[:, b::2, :], banks[b][:, :].rearrange("p (h n) -> p h n", h=HP),
                                        0.125, None, ALU.mult).then_inc(split, 1)
                nc.vector.tensor_scalar(btmp[:, b::2, :], banks[2 + b][:, :].rearrange("p (h n) -> p h n", h=HP),
                                        0.125, None, ALU.mult).then_inc(split, 1)
                nc.vector.tensor_copy(wz[:, b::2, :], z_half(b)).then_inc(split, 1)
            dve.wait_ge(split, 6)
            nc.vector.tensor_copy(w1[:, :, :], wtmp[:, :, :]).then_inc(split, 1)
            nc.vector.tensor_copy(bhi[:, :, :], btmp[:, :, :]).then_inc(split, 1)
            for b in range(2):
                nc.vector.tensor_tensor(wz[CC:P, b::2, :], z_half(b)[CC:P], wz[CC:P, b::2, :].bitcast(FP32),
                                        ALU.subtract).then_inc(split, 1)
            dve.wait_ge(split, 10)
            nc.vector.tensor_copy(w2[0:CC, :, :], wtmp[0:CC, :, :]).then_inc(split, 1)
            nc.vector.tensor_tensor(w1[CC:P, :, :], wtmp[CC:P, :, :], w1[CC:P, :, :].bitcast(FP32), ALU.subtract)\
                .then_inc(split, 1)
            nc.vector.tensor_tensor(bres[:, :, :], btmp[:, :, :], bhi[:, :, :].bitcast(FP32), ALU.subtract)\
                .then_inc(split, 1)
            dve.wait_ge(split, 13)
            nc.vector.tensor_scalar(btmp[:, :, :], bhi[:, :, :].bitcast(FP32), is_hi, None, ALU.mult).then_inc(split, 1)
            dve.wait_ge(split, 14)
            nc.vector.scalar_tensor_tensor(w2[CC:P, :, :], bres[CC:P, :, :], is_lo[CC:P, :], btmp[CC:P, :, :],
                                           ALU.mult, ALU.add).then_inc(split, 1)
            nc.vector.tensor_tensor(out_bias[:, :], par0("bo"), banks[7][:, 0:1], ALU.add).then_inc(split, 1)
            dve.wait_ge(split, 16)
            dve.sem_inc(weights_ready, 1)
            lower_part(0, 0)
            affine(1, 1, 1)

            def row_max(g, u):
                s = u % 2
                dve.wait_ge(scores_ready, g + 1)
                for h in range(2):
                    ins = nc.vector.tensor_reduce(neg_max[:, s, 2 * h:2 * h + 2], shape3(scores[s][h]),
                                                  mybir.AxisListType.X, ALU.max, negate=True)
                ins.then_inc(max_ready, 1)

            def invert_sums(g, u):
                s = u % 2
                dve.wait_ge(probs_ready, 4 * g + 4)
                nc.vector.reciprocal(recip[:, s, :], sums[:, s, :]).then_inc(recip_ready, 1)

            def copy_pT(g, h):
                dve.wait_ge(turned_ready, 2 * g + (h + 1))
                nc.vector.tensor_copy(pT[:, h, :, :], shape3(turned)).then_inc(pT_ready, 1)

            def take_lo(n, v):
                dve.wait_ge(qq_hi, U * n + (v + 1))
                bank = bank_of(("qq", v))
                slot = qq[CC:P, v, :, :]
                nc.vector.tensor_tensor(slot, shape3(bank)[CC:P], slot.bitcast(FP32), ALU.subtract)\
                    .then_inc(qq_ready, 1)

            for v in range(U):
                take_lo(0, v)
            lower_part(1, 1)
            row_max(0, 0)
            row_max(1, 1)
            invert_sums(0, 0)

            def body(i, last):
                for s in range(2):
                    m = 2 * i + s
                    for v in range(U):
                        g = 2 * U * i + (U * s + v)
                        left = 2 * U - (U * s + v) if last else 2 * U
                        if left > 1:
                            invert_sums(g + 1, v + 1)
                        copy_pT(g, 0)
                        if left > 2:
                            row_max(g + 2, v)
                        copy_pT(g, 1)
                        if not (last and s == 1):
                            take_lo(m + 1, v)
                        if v == 2 and not last:
                            affine(m + 2, s, i + 2)
                        if v == 3 and not last:
                            lower_part(m + 2, s)
                    dve.wait_ge(acc_ready, m + 1)
                    nc.vector.tensor_copy(o[:, :, s * CC:(s + 1) * CC], acc[s]).then_inc(o_ready, 1)
                dve.wait_ge(out_ready, i + 1)
                xi = X[:, bass.ds(i, 1), :].rearrange("p a n -> p (a n)")
                nc.vector.scalar_tensor_tensor(xi, out_T, out_bias[:, 0:1], xi, ALU.add, ALU.add)

            with dve.Fori(0, PAIRS - 1) as i:
                body(i, False)
            body(PAIRS - 1, True)

        @block.scalar
        def _(act):
            act.dma_start(p0[:, :], params0).then_inc(loaded_params, 16)
            act.dma_start(params_sb[:, :], params).then_inc(loaded_params, 16)
            act.wait_ge(eps_set, 1)
            act.wait_ge(gn_vars, 1)
            nc.scalar.activation(rstd[:, :], misc[0][:, 2 * B:3 * B], ACT.Ln, bias=eps[:, 0:1]).then_inc(gn_log, 1)
            act.wait_ge(gn_log, 1)
            nc.scalar.activation(rstd[:, :], rstd[:, :], ACT.Exp, scale=-0.5).then_inc(gn_rstd, 1)

            def exps(g, u):
                s = u % 2
                act.wait_ge(max_ready, g + 1)
                for h in range(2):
                    if h == 1 and not isinstance(g, int) or h == 1 and g >= 2:
                        act.wait_ge(turned_ready, 2 * (g - 1))
                    for q in range(QT):
                        n = 2 * h + q
                        nc.scalar.activation(probs[:, s, h, q, :], scores[s][h][:, q * C:(q + 1) * C], ACT.Exp,
                                             bias=neg_max[:, s, n:n + 1], accum_out=sums[:, s, n:n + 1])\
                            .then_inc(probs_ready, 1)

            def take(n, par, item):
                kind, v = item
                bank = bank_of(item)
                if kind == "qq":
                    act.wait_ge(qq_full, U * n + (v + 1))
                    nc.scalar.copy(qq[:, v, :, :], bank[:, :].rearrange("p (a n) -> p a n", a=2)).then_inc(qq_hi, 1)
                else:
                    act.wait_ge(z_full, QT * n + (v + 1))
                    nc.scalar.copy(z[par][:, v, :], bank[:, :]).then_inc(z_ready, 1)

            for v in range(U):
                for item in ITEMS[v]:
                    take(0, 0, item)
            exps(0, 0)
            exps(1, 1)

            def body(i, last):
                for s in range(2):
                    for v in range(U):
                        g = 2 * U * i + (U * s + v)
                        if not last or U * s + v + 2 < 2 * U:
                            exps(g + 2, v)
                        if not (last and s == 1):
                            for item in ITEMS[v]:
                                take(2 * i + (s + 1), 1 - s, item)

            with act.Fori(0, PAIRS - 1) as i:
                body(i, False)
            body(PAIRS - 1, True)

        @block.tensor
        def _(pe):
            pe.wait_ge(loaded_params, 32)
            for h in range(H):
                hp, rows = h // 2, slice(CC * (h % 2), CC * (h % 2) + CC)
                cols = slice(hp * P, hp * P + P)
                nc.tensor.matmul(banks[h % 2][:, cols], wqn[rows, hp, :], wkn[rows, hp, :], start=True, stop=True)
                nc.tensor.matmul(banks[2 + h % 2][:, cols], bqz[rows, hp, :], wkn[rows, hp, :], start=True, stop=True)
                nc.tensor.matmul(z_half(h % 2)[:, hp, :], wvn[rows, hp, :], wo[rows, hp, :],
                                 start=True, stop=True)
            for smp in range(2):
                for hp in range(HP):
                    ins = nc.tensor.matmul(banks[7][CC * smp:CC * smp + CC, 0:1], wo[:, hp, :], bv[:, hp:hp + 1],
                                           start=hp == 0, stop=hp == HP - 1)
            ins.then_inc(folded, 1)
            pe.wait_ge(stats_done, 2 * PAIRS)
            by_sample = [misc[0][:, (1 + k) * B:(2 + k) * B].rearrange("p (i s) -> p i s", s=2) for k in range(2)]
            nc.tensor.matmul(misc[0][:, 0:PAIRS], par0("mean64"), moments[:, :, 0], start=True, stop=True)
            for s in range(2):
                ins = nc.tensor.matmul(by_sample[0][:, :, s], pick[:, s, :], moments[:, :, 0], start=True, stop=True)
            ins.then_inc(gn_means, 1)
            pe.wait_ge(gn_offsets, 3)
            for s in range(2):
                ins = nc.tensor.matmul(by_sample[1][:, :, s], pick[:, s, :], spread[:, :], start=True, stop=True)
            ins.then_inc(gn_vars, 1)

            def product(n, par, item):
                kind, v = item
                bank = bank_of(item)
                first = isinstance(n, int) and n == 0
                if item == ("qq", 0) and not first:
                    pe.wait_ge(z_ready, QT * (n - 1) + 2)
                if item == ("qq", 1) and not first:
                    pe.wait_ge(qq_ready, U * (n - 1) + 4)
                if item == ("z", 0):
                    pe.wait_ge(qq_ready, U * n + 1)
                if item == ("qq", 2):
                    pe.wait_ge(qq_ready, U * n + 2)
                if item == ("z", 1):
                    pe.wait_ge(z_ready, QT * n + 1)
                if item == ("qq", 3):
                    pe.wait_ge(qq_ready, U * n + 3)
                if v == 0:
                    pe.wait_ge(prepared, n + 1)
                    pe.wait_ge(x_parts, n + 1)
                if kind == "qq":
                    for h in range(2):
                        out = bank[:, h * C:(h + 1) * C]
                        nc.tensor.matmul(out, w1[:, 2 * v + h, :], x1[par][:, :], start=True, stop=False)
                        ins = nc.tensor.matmul(out, w2[:, 2 * v + h, :], x2[par][:, :], start=False, stop=True)
                    ins.then_inc(qq_full, 1)
                else:
                    cols = slice(v * P, (v + 1) * P)
                    nc.tensor.matmul(bank[:, :], c1[par][:, cols], wz[:, :, :], start=True, stop=False)
                    nc.tensor.matmul(bank[:, :], c2[par][:, cols], wz[:, :, :], start=False, stop=True)\
                        .then_inc(z_full, 1)

            def score(g, par, v):
                pe.wait_ge(qq_ready, g + 1)
                if not isinstance(g, int) or g >= 2:
                    pe.wait_ge(probs_ready, 4 * (g - 1))
                for h in range(2):
                    for q in range(QT):
                        out = scores[v % 2][h][:, q * C:(q + 1) * C]
                        w = qq[:, v, h, q * P:(q + 1) * P]
                        nc.tensor.matmul(out, w, c1[par][:, :], start=True, stop=False)
                        ins = nc.tensor.matmul(out, w, c2[par][:, :], start=False, stop=True)
                ins.then_inc(scores_ready, 1)

            def turn(g, v, h):
                pe.wait_ge(norm_ready, 4 * g + (2 * h + 2))
                pe.wait_ge(pT_ready, 2 * g + (h + 1))
                for k in range(QT):
                    for q in range(QT):
                        ins = nc.tensor.transpose(turned[:, k * C + q * P:k * C + q * P + P],
                                                  probs[:, v % 2, h, q, k * P:(k + 1) * P], ident)
                ins.then_inc(turned_ready, 1)

            def attend(g, s, v, h):
                pe.wait_ge(pT_ready, 2 * g + (h + 2))
                for k in range(QT):
                    for q in range(QT):
                        head = 2 * v + h
                        ins = nc.tensor.matmul(acc[s][:, q, :], pT[:, h, k, q * P:(q + 1) * P],
                                               z[s][:, k, head * CC:(head + 1) * CC],
                                               start=head == 0 and k == 0 and q == 0,
                                               stop=head == H - 1 and k == QT - 1, skip_group_check=True)
                return ins

            pe.wait_ge(weights_ready, 1)
            for v in range(U):
                for item in ITEMS[v]:
                    product(0, 0, item)
            score(0, 0, 0)
            score(1, 0, 1)

            def body(i, last):
                for s in range(2):
                    m = 2 * i + s
                    for v in range(U):
                        g = 2 * U * i + (U * s + v)
                        turn(g, v, 0)
                        if not last or U * s + v + 2 < 2 * U:
                            score(g + 2, s if v < 2 else 1 - s, (v + 2) % U)
                        turn(g, v, 1)
                        if v == 0:
                            pe.wait_ge(z_ready, 2 * QT * i + QT * (s + 1))
                        attend(g, s, v, 0)
                        if v < U - 1 and not (last and s == 1):
                            for item in ITEMS[v]:
                                product(m + 1, 1 - s, item)
                        ins = attend(g, s, v, 1)
                        if v == U - 1:
                            ins.then_inc(acc_ready, 1)
                            if not (last and s == 1):
                                for item in ITEMS[v]:
                                    product(m + 1, 1 - s, item)
                pe.wait_ge(o_ready, 2 * i + 2)
                for q in range(QT):
                    ins = nc.tensor.transpose(out_T[:, q * P:(q + 1) * P], o[:, q, :], ident)
                ins.then_inc(out_ready, 1)

            with pe.Fori(0, PAIRS - 1) as i:
                body(i, False)
            body(PAIRS - 1, True)


@buffers
def layer1(nc, sb, sem, par, banks, X, shift_sb, state_sb, eps, out):
    ident, ones8, mean8 = par("ident"), par("ones8"), par("mean8")
    spread, gather = par("spread", HS, P), par("gather", HS, P)
    maa_w1, maa_w2, maa_w2g = par("maa_w1", CT, MAA * MD), par("maa_w2"), par("maa_w2g")
    decay_w1, decay_w2 = par("decay_w1", CT, DD), par("decay_w2")
    W = {n: par(n, CT, C) for n in SQUARES}
    vec = {n: par(n) for n in VECTORS}

    stat = sb("stat", [P, TT, 6])
    mom = sb("mom", [P, TT, 2])
    rstd = sb("rstd", [P, TT])
    xh = sb("xh", [P, TT, C])
    xa = sb("xa", [P, CT, G, L + 1])
    sx = sb("sx", [P, CT, GT])
    xx = sb("xx", [P, CT, GT])
    low1 = sb("low1", [P, GT])
    low2 = sb("low2", [MD, GT])
    xj = [sb(f"xj{j}", [P, CT, GT]) for j in range(MAA)]
    dh = sb("dh", [DD, GT])
    we = sb("we", [P, CT, GT])
    wd = sb("wd", [P, CT, G, L])
    r = sb("r", [P, CT, GT])
    k = sb("k", [P, CT, GT])
    v1 = sb("v1", [P, CT, GT])
    g = sb("g", [P, CT, GT])
    RING = 4
    a = sb("a", [P, RING, G, L])
    s = sb("s", [P, RING, GT])
    rs = sb("rs", [P, RING, GT])
    ruk = sb("ruk", [P, CT, GT])
    yc = sb("yc", [P, CT, GT])
    yd = sb("yd", [P, CT, GT])
    x2 = sb("x2", [P, TT, C])

    names = ["go", "col0", "st", "mo", "lg", "rs_", "xh", "xT", "xa", "sx", "xx", "low", "tanh", "mix", "mixt", "xj",
             "proj", "evac", "wdec", "sig", "gate", "vb", "a0", "a", "s", "rs", "y", "ruk", "q", "qv", "yc", "gm", "yd",
             "sq", "var", "lnv", "grs", "n1", "n2", "yg", "o", "x2", "fx", "fk", "fr", "kk", "kr", "kq", "rr", "rg",
             "f", "fm", "out", "stored", "group_free"]
    S = {n: sem("l1_" + n) for n in names}

    def grouped(t):
        return t.rearrange("p (b l) -> p b l", b=G)

    PROJ = [("dec1", 0), ("k", 0), ("k", 1), ("dec2", 0), ("dec2", 1), ("r", 0), ("r", 1), ("v", 0), ("v", 1),
            ("g", 0), ("g", 1)]
    NP = len(PROJ)
    NE = NP - 2
    MIX = [(j, c) for j in (0, 1, 3, 2, 4) for c in range(CT)]
    SRC = {"dec1": 0, "k": 1, "v": 2, "r": 3, "g": 4}
    STEPS = [(c, t) for c in range(CT) for t in range(HS)]
    NS = len(STEPS)

    with nc.Block() as block:
        @block.sync
        def _(sp):
            sp.sem_inc(S["group_free"], 1)
            with sp.Fori(0, GROUPS) as i:
                sp.wait_ge(S["out"], TT // 2 * (i + 1))
                sp.dma_start(out[:, bass.ds(i * TT, TT), :], xh[:, :, :]).then_inc(S["stored"], 16)
                sp.wait_ge(S["stored"], 16 * (i + 1))
                sp.sem_inc(S["group_free"], 1)

        @block.gpsimd
        def _(pool):
            ins = nc.gpsimd.memset(wd[:, :, :, 0:1], 0.0)
            with pool.Fori(0, GROUPS) as i:
                def col0(which, n):
                    for c in range(CT):
                        ins = nc.gpsimd.tensor_copy(xa[:, c, :, 0], shift_sb[:, which, c, bass.ds(i * G, G)])
                        ins.then_inc(S["col0"], 1)

                def diff(n):
                    for c in range(CT):
                        pool.wait_ge(S["xa"], 2 * CT * i + n * CT + c + 1)
                        if c == 0:
                            pool.wait_ge(S["col0"], 2 * CT * i + (n + 1) * CT)
                        nc.gpsimd.tensor_tensor(grouped(sx[:, c, :]), xa[:, c, :, 0:L], xa[:, c, :, 1:L + 1],
                                                ALU.subtract).then_inc(S["sx"], 1)

                pool.wait_ge(S["group_free"], i + 1)
                col0(1, 0)
                diff(0)
                for n, (j, c) in enumerate(MIX):
                    pool.wait_ge(S["mixt"], len(MIX) * i + n + 1)
                    nc.gpsimd.tensor_tensor(grouped(xj[j][:, c, :]), grouped(xj[j][:, c, :]), xa[:, c, :, 1:L + 1],
                                            ALU.add).then_inc(S["xj"], 1)
                for n, (c, t) in enumerate(STEPS):
                    if n < RING:
                        nc.gpsimd.tensor_copy(a[:, n % RING, :, 0], state_sb[:, c, t, bass.ds(i * G, G)])\
                            .then_inc(S["a0"], 1)
                if True:
                    for n, (c, t) in enumerate(STEPS):
                        m = n % RING
                        pool.wait_ge(S["s"], NS * i + n + 1)
                        if n + RING < NS:
                            cn, tn = STEPS[n + RING]
                            nc.gpsimd.tensor_copy(a[:, m, :, 0], state_sb[:, cn, tn, bass.ds(i * G, G)])\
                                .then_inc(S["a0"], 1)
                        pool.wait_ge(S["evac"], NE * i + 7)
                        if n >= RING:
                            pool.wait_ge(S["y"], NS * i + (n - RING + 1))
                        nc.gpsimd.tensor_tensor(rs[:, m, :], r[:, c, :], s[:, m, :], ALU.mult).then_inc(S["rs"], 1)
                pool.wait_ge(S["x2"], 2 * (i + 1))
                col0(0, 1)
                diff(1)
                for c in range(CT):
                    pool.wait_ge(S["kr"], CT * i + c + 1)
                    nc.gpsimd.tensor_tensor(xj[2][:, c, :], we[:, c, :], we[:, c, :], ALU.mult).then_inc(S["kq"], 1)
                for b in range(2):
                    pool.wait_ge(S["fm"], 2 * i + b + 1)
                    nc.gpsimd.tensor_tensor(xh[:, 2 * b:2 * b + 2, :], yd[:, b, :].rearrange("p (a n) -> p a n", a=2),
                                            x2[:, 2 * b:2 * b + 2, :], ALU.add).then_inc(S["out"], 1)

        @block.vector
        def _(dve):
            with dve.Fori(0, GROUPS) as i:
                dve.wait_ge(S["group_free"], i + 1)

                def layernorm(n, tile):
                    for j in range(TT):
                        nc.vector.bn_stats(stat[:, j, :], tile(j)).then_inc(S["st"], 1)
                    dve.wait_ge(S["st"], 2 * TT * i + (n + 1) * TT)
                    dve.sem_inc(S["go"], 1)
                    for j in range(TT):
                        nc.vector.bn_aggr(mom[:, j, :], stat[:, j, :]).then_inc(S["mo"], 1)
                    dve.wait_ge(S["rs_"], 2 * i + n + 1)
                    for j in range(TT):
                        nc.vector.tensor_scalar(xh[:, j, :], tile(j), mom[:, j, 0:1], rstd[:, j:j + 1],
                                                ALU.subtract, ALU.mult).then_inc(S["xh"], 1)

                layernorm(0, lambda j: X[:, bass.ds(i * TT + j, 1), :].rearrange("p a n -> p (a n)"))
                for c in range(CT):
                    dve.wait_ge(S["sx"], 2 * CT * i + c + 1)
                    nc.vector.scalar_tensor_tensor(grouped(xx[:, c, :]), grouped(sx[:, c, :]),
                                                   vec["maa_x"][:, c:c + 1], xa[:, c, :, 1:L + 1],
                                                   ALU.mult, ALU.add).then_inc(S["xx"], 1)
                maa = ["maa_w", "maa_k", "maa_v", "maa_r", "maa_g"]
                for n, (j, c) in enumerate(MIX):
                    dve.wait_ge(S["mix"], len(MIX) * i + n + 1)
                    nc.vector.scalar_tensor_tensor(xj[j][:, c, :], banks[4 + n % 4][:, :], vec[maa[j]][:, c:c + 1],
                                                   sx[:, c, :], ALU.add, ALU.mult).then_inc(S["mixt"], 1)
                for c in range(CT):
                    dve.wait_ge(S["evac"], NE * i + 6 + c)
                    nc.vector.scalar_tensor_tensor(ruk[:, c, :], k[:, c, :], vec["faaaa"][:, c:c + 1], r[:, c, :],
                                                   ALU.mult, ALU.mult).then_inc(S["ruk"], 1)
                def gates():
                    for c in range(CT):
                        dve.wait_ge(S["sig"], CT * i + c + 1)
                        nc.vector.tensor_tensor(g[:, c, :], banks[(9 + c) % 4][:, :], g[:, c, :], ALU.mult)\
                            .then_inc(S["gate"], 1)
                gates()
                dve.wait_ge(S["wdec"], CT * (i + 1))
                for n, (c, t) in enumerate(STEPS):
                    m = n % RING
                    dve.wait_ge(S["vb"], NS * i + n + 1)
                    nc.vector.tensor_tensor(a[:, m, :, 1:L], grouped(banks[4 + m][:, :])[:, :, 0:L - 1],
                                            grouped(k[:, c, :])[:, :, 0:L - 1], ALU.mult).then_inc(S["a"], 1)
                    dve.wait_ge(S["a"], NS * i + n + 1)
                    dve.wait_ge(S["a0"], NS * i + n + 1)
                    if n >= RING:
                        dve.wait_ge(S["rs"], NS * i + (n - RING + 1))
                    nc.vector.tensor_tensor_scan(s[:, m, :], wd[:, c, :, :].rearrange("p b l -> p (b l)"),
                                                 a[:, m, :, :].rearrange("p b l -> p (b l)"), 0.0,
                                                 ALU.mult, ALU.add).then_inc(S["s"], 1)
                for c in range(CT):
                    dve.wait_ge(S["q"], CT * i + c + 1)
                    nc.vector.tensor_tensor(yd[:, c, :], banks[2 + c][:, :], v1[:, c, :], ALU.mult).then_inc(S["qv"], 1)
                for c in range(CT):
                    dve.wait_ge(S["qv"], CT * i + c + 1)
                    dve.wait_ge(S["y"], NS * i + (c + 1) * HS)
                    nc.vector.tensor_tensor(yc[:, c, :], banks[c][:, :], yd[:, c, :], ALU.add).then_inc(S["yc"], 1)
                for c in range(CT):
                    dve.wait_ge(S["gm"], CT * i + c + 1)
                    nc.vector.tensor_tensor(yd[:, c, :], yc[:, c, :], banks[2 + c][:, :], ALU.subtract)\
                        .then_inc(S["yd"], 1)
                for c in range(CT):
                    dve.wait_ge(S["grs"], CT * i + c + 1)
                    nc.vector.tensor_tensor(yd[:, c, :], yd[:, c, :], yc[:, c, :], ALU.mult).then_inc(S["n1"], 1)
                for c in range(CT):
                    dve.wait_ge(S["n1"], CT * i + c + 1)
                    nc.vector.tensor_scalar(yd[:, c, :], yd[:, c, :], vec["gn_w"][:, c:c + 1], vec["gn_b"][:, c:c + 1],
                                            ALU.mult, ALU.add).then_inc(S["n2"], 1)
                for c in range(CT):
                    dve.wait_ge(S["n2"], CT * i + c + 1)
                    nc.vector.tensor_tensor(yc[:, c, :], yd[:, c, :], g[:, c, :], ALU.mult).then_inc(S["yg"], 1)
                for b in range(2):
                    dve.wait_ge(S["o"], 2 * i + b + 1)
                    nc.vector.tensor_tensor(x2[:, 2 * b:2 * b + 2, :], banks[4 + b][:, :].rearrange("p (a n) -> p a n", a=2),
                                            X[:, bass.ds(i * TT + 2 * b, 2), :], ALU.add).then_inc(S["x2"], 1)
                dve.wait_ge(S["x2"], 2 * (i + 1))
                layernorm(1, lambda j: x2[:, j, :])
                for c in range(CT):
                    dve.wait_ge(S["sx"], 2 * CT * i + CT + c + 1)
                    for which, (name, done) in enumerate((("fmaa_k", "fk"), ("fmaa_r", "fr"))):
                        nc.vector.scalar_tensor_tensor(grouped(xj[which][:, c, :]), grouped(sx[:, c, :]),
                                                       vec[name][:, c:c + 1], xa[:, c, :, 1:L + 1],
                                                       ALU.mult, ALU.add).then_inc(S[done], 1)
                for b in range(2):
                    dve.wait_ge(S["f"], 2 * i + b + 1)
                    dve.wait_ge(S["rg"], 2 * i + b + 1)
                    nc.vector.tensor_tensor(yd[:, b, :], banks[4 + b][:, :], yc[:, b, :], ALU.mult)\
                        .then_inc(S["fm"], 1)

        @block.scalar
        def _(act):
            with act.Fori(0, GROUPS) as i:
                act.wait_ge(S["group_free"], i + 1)

                def rstds(n):
                    act.wait_ge(S["mo"], 2 * TT * i + (n + 1) * TT)
                    nc.scalar.activation(rstd[:, :], mom[:, :, 1], ACT.Ln, bias=eps[:, 0:1]).then_inc(S["lg"], 1)
                    act.wait_ge(S["lg"], 2 * i + n + 1)
                    nc.scalar.activation(rstd[:, :], rstd[:, :], ACT.Exp, scale=-0.5).then_inc(S["rs_"], 1)

                def affine(n, w, b, bank):
                    for c in range(CT):
                        act.wait_ge(S["xT"], 2 * CT * i + n * CT + c + 1)
                        nc.scalar.activation(xa[:, c, :, 1:L + 1], grouped(banks[bank + c][:, :]), ACT.Identity,
                                             scale=vec[w][:, c:c + 1], bias=vec[b][:, c:c + 1]).then_inc(S["xa"], 1)

                rstds(0)
                affine(0, "ln1_w", "ln1_b", 0)
                act.wait_ge(S["low"], 2 * i + 1)
                nc.scalar.activation(low1[:, :], banks[2][:, :], ACT.Tanh).then_inc(S["tanh"], 1)
                act.wait_ge(S["low"], 2 * i + 2)
                nc.scalar.activation(low2[:, :], banks[3][0:MD, :], ACT.Tanh).then_inc(S["tanh"], 1)
                dst = {"k": k, "r": r, "v": v1}
                for n, (name, c) in enumerate(PROJ):
                    act.wait_ge(S["proj"], NP * i + n + 1)
                    bank = banks[n % 4]
                    if name == "dec1":
                        nc.scalar.activation(dh[:, :], bank[0:DD, :], ACT.Tanh).then_inc(S["evac"], 1)
                    elif name == "dec2":
                        nc.scalar.activation(we[:, c, :], bank[:, :], ACT.Exp, bias=vec["time_decay"][:, c:c + 1])\
                            .then_inc(S["evac"], 1)
                        act.wait_ge(S["evac"], NE * i + n + 1)
                        nc.scalar.activation(wd[:, c, :, 1:L], grouped(we[:, c, :])[:, :, 0:L - 1], ACT.Exp, scale=-1.0)\
                            .then_inc(S["wdec"], 1)
                    elif name == "g":
                        nc.scalar.activation(g[:, c, :], bank[:, :], ACT.Sigmoid).then_inc(S["sig"], 1)
                    else:
                        nc.scalar.copy(dst[name][:, c, :], bank[:, :]).then_inc(S["evac"], 1)
                for c in range(CT):
                    act.wait_ge(S["yd"], CT * i + c + 1)
                    nc.scalar.activation(xx[:, c, :], yd[:, c, :], ACT.Square).then_inc(S["sq"], 1)
                for c in range(CT):
                    act.wait_ge(S["var"], CT * i + c + 1)
                    nc.scalar.activation(xx[:, c, :], banks[c][:, :], ACT.Ln, bias=eps[:, 0:1]).then_inc(S["lnv"], 1)
                for c in range(CT):
                    act.wait_ge(S["lnv"], CT * i + c + 1)
                    nc.scalar.activation(yc[:, c, :], xx[:, c, :], ACT.Exp, scale=-0.5).then_inc(S["grs"], 1)
                rstds(1)
                affine(1, "ln2_w", "ln2_b", 6)
                for c in range(CT):
                    act.wait_ge(S["kk"], CT * i + c + 1)
                    nc.scalar.activation(we[:, c, :], banks[c][:, :], ACT.Relu).then_inc(S["kr"], 1)
                for b in range(2):
                    act.wait_ge(S["rr"], 2 * i + b + 1)
                    nc.scalar.activation(yc[:, b, :], banks[2 + b][:, :], ACT.Sigmoid).then_inc(S["rg"], 1)

        @block.tensor
        def _(pe):
            with pe.Fori(0, GROUPS) as i:
                pe.wait_ge(S["group_free"], i + 1)

                def turn(n, bank):
                    for c in range(CT):
                        for j in range(TT):
                            if c == 0:
                                pe.wait_ge(S["xh"], 2 * TT * i + n * TT + j + 1)
                            ins = nc.tensor.transpose(banks[bank + c][:, j * P:(j + 1) * P], xh[:, j, c * P:(c + 1) * P],
                                                      ident)
                        ins.then_inc(S["xT"], 1)

                def product(bank, w, src, co):
                    for ci in range(CT):
                        ins = nc.tensor.matmul(bank, w[:, ci, co], src[:, ci, :], start=ci == 0, stop=ci == CT - 1)
                    return ins

                def token_product(b, w, src, bank):
                    for j in range(2):
                        tok = slice((2 * b + j) * P, (2 * b + j + 1) * P)
                        for ci in range(CT):
                            ins = nc.tensor.matmul(banks[bank + b][:, j * C:(j + 1) * C], src[:, ci, tok], w[:, ci, :],
                                                   start=ci == 0, stop=ci == CT - 1)
                    return ins

                turn(0, 0)
                pe.wait_ge(S["xx"], CT * (i + 1))
                product(banks[2][:, :], maa_w1, xx, slice(0, P)).then_inc(S["low"], 1)
                product(banks[3][0:MD, :], maa_w1, xx, slice(P, P + MD)).then_inc(S["low"], 1)
                for n, (j, c) in enumerate(MIX):
                    pe.wait_ge(S["tanh"], 2 * i + (2 if j == 4 else 1))
                    if n >= 4:
                        pe.wait_ge(S["mixt"], len(MIX) * i + (n - 3))
                    w, src, at = (maa_w2g, low2, 0) if j == 4 else (maa_w2, low1, MD * j)
                    nc.tensor.matmul(banks[4 + n % 4][:, :], w[at:at + MD, c * P:(c + 1) * P], src[at:at + MD, :],
                                     start=True, stop=True).then_inc(S["mix"], 1)
                order = [j for j, c in MIX if c == 1]
                for n, (name, c) in enumerate(PROJ):
                    if n >= 4:
                        pe.wait_ge(S["evac"], NE * i + (n - 3))
                    if n == 0:
                        pe.wait_ge(S["tanh"], 2 * (i + 1))
                    bank = banks[n % 4]
                    if name == "dec2":
                        pe.wait_ge(S["evac"], NE * i + 1)
                        ins = nc.tensor.matmul(bank[:, :], decay_w2[0:DD, c * P:(c + 1) * P], dh[:, :],
                                               start=True, stop=True)
                    else:
                        j = SRC[name]
                        pe.wait_ge(S["xj"], len(MIX) * i + CT * (order.index(j) + 1))
                        if name == "dec1":
                            ins = product(bank[0:DD, :], decay_w1, xj[j], slice(0, DD))
                        else:
                            ins = product(bank[:, :], W["W" + name], xj[j], slice(c * P, (c + 1) * P))
                    ins.then_inc(S["proj"], 1)

                pe.wait_ge(S["mixt"], len(MIX) * (i + 1))
                pe.wait_ge(S["evac"], NE * (i + 1))

                def spread_v(n):
                    c, t = STEPS[n]
                    if n >= RING:
                        pe.wait_ge(S["a"], NS * i + (n - RING + 1))
                    nc.tensor.matmul(banks[4 + n % RING][:, :], spread[:, t, :], v1[:, c, :], start=True, stop=True)\
                        .then_inc(S["vb"], 1)

                def sum_rs(n):
                    c, t = STEPS[n]
                    pe.wait_ge(S["rs"], NS * i + n + 1)
                    nc.tensor.matmul(banks[c][:, :], gather[:, t, :], rs[:, n % RING, :], start=t == 0,
                                     stop=t == HS - 1).then_inc(S["y"], 1)

                for n in range(RING):
                    spread_v(n)
                pe.wait_ge(S["gate"], CT * (i + 1))
                for c in range(CT):
                    pe.wait_ge(S["ruk"], CT * i + c + 1)
                    nc.tensor.matmul(banks[2 + c][:, :], ones8, ruk[:, c, :], start=True, stop=True).then_inc(S["q"], 1)
                for n in range(NS):
                    if n + RING < NS:
                        spread_v(n + RING)
                    sum_rs(n)
                for c in range(CT):
                    pe.wait_ge(S["yc"], CT * i + c + 1)
                    nc.tensor.matmul(banks[2 + c][:, :], mean8, yc[:, c, :], start=True, stop=True).then_inc(S["gm"], 1)
                for c in range(CT):
                    pe.wait_ge(S["sq"], CT * i + c + 1)
                    nc.tensor.matmul(banks[c][:, :], mean8, xx[:, c, :], start=True, stop=True).then_inc(S["var"], 1)
                pe.wait_ge(S["yg"], CT * (i + 1))
                for b in range(2):
                    token_product(b, W["Wo"], yc, 4).then_inc(S["o"], 1)
                turn(1, 6)
                pe.wait_ge(S["fk"], CT * (i + 1))
                for c in range(CT):
                    product(banks[c][:, :], W["fWk"], xj[0], slice(c * P, (c + 1) * P)).then_inc(S["kk"], 1)
                pe.wait_ge(S["fr"], CT * (i + 1))
                for b in range(2):
                    token_product(b, W["fWr"], xj[1], 2).then_inc(S["rr"], 1)
                pe.wait_ge(S["kq"], CT * (i + 1))
                for b in range(2):
                    token_product(b, W["fWv"], xj[2], 4).then_inc(S["f"], 1)


def constants():
    p = np.arange(P)
    head = p[:, None] // HS == p[None, :] // HS
    spread = np.stack([(head & (p[:, None] % HS == t)) for t in range(HS)], 1).astype(np.float32)
    gather = np.stack([(head & (p[None, :] % HS == t)) for t in range(HS)], 1).astype(np.float32)
    head = head.astype(np.float32)
    return {"ident": np.eye(P, dtype=np.float32), "ones8": head,
            "mean8": head / np.float32(HS), "spread": spread.reshape(P, -1), "gather": gather.reshape(P, -1)}


def constants0():
    p = np.arange(P)
    sample = (p[:, None] // CC == p[None, :] // CC).astype(np.float32)
    pick = np.stack([np.broadcast_to((p // CC == s)[:, None], (P, P)) for s in range(2)], 1).astype(np.float32)
    return {"mean64": sample / np.float32(CC), "pick": pick.reshape(P, -1) / np.float32(CC),
            "is_hi": (p == CC).astype(np.float32)[:, None], "is_lo": (p == CC + 1).astype(np.float32)[:, None]}


def tiles(a):
    return a.reshape(-1, P, a.shape[1]).transpose(1, 0, 2).reshape(P, -1)


def pack0(inputs):
    def l0(name):
        return np.asarray(inputs["L0_xattn_" + name])

    def twice(a):
        return np.concatenate([a, a], 0)

    def doubled(w):
        return tiles(np.concatenate([w, w], 1))

    bqz = np.zeros((P, HP, P), np.float32)
    bqz[:, :, CC] = l0("bq").reshape(HP, P).T
    bqz[:, :, CC + 1] = l0("bq").reshape(HP, P).T
    f = {"wqn": doubled(l0("Wq")), "wkn": doubled(l0("Wkv")[:HP * P]), "wvn": doubled(l0("Wkv")[HP * P:]),
         "bqz": bqz.reshape(P, -1), "wo": tiles(l0("Wo").T), "bv": l0("bkv")[HP * P:].reshape(HP, P).T,
         "gamma": twice(l0("gamma")[:, None]), "beta": twice(l0("beta")[:, None]), "bo": twice(l0("bo")[:, None]),
         **constants0()}
    return np.ascontiguousarray(np.concatenate([f[name] for name, _ in FIELDS0], 1))


def pack(inputs):
    def l1(name):
        return np.asarray(inputs["L1_xattn_" + name])

    def padded(a):
        full = np.zeros((P, a.shape[1]), a.dtype)
        full[:a.shape[0]] = a
        return full

    f = {"maa_w1": tiles(l1("maa_w1")), "maa_w2": l1("maa_w2")[:4].reshape(P, C), "maa_w2g": padded(l1("maa_w2")[4]),
         "decay_w1": tiles(l1("decay_w1")), "decay_w2": padded(l1("decay_w2")), **constants()}
    for name in VECTORS:
        f[name] = l1(name).reshape(CT, P).T
    for name in SQUARES:
        f[name] = tiles(l1(name).T)
    return np.ascontiguousarray(np.concatenate([f[name] for name, _ in FIELDS], 1))


def kernel(**inputs):
    import concourse.bacc as bacc
    from concourse.bass_utils import run_bass_kernel_spmd

    x = np.ascontiguousarray(np.asarray(inputs["x"]))
    context = np.ascontiguousarray(np.asarray(inputs["ctx_2048"]))
    shift = np.ascontiguousarray(context[:, 0:2].reshape(B, 2, CT, P).transpose(3, 1, 2, 0))
    state = np.ascontiguousarray(context[:, 2:2 + HS].reshape(B, CT, P, HS).transpose(2, 1, 3, 0))
    arrays = {"x_dram": x, "ctx_dram": context, "params_dram": pack(inputs), "params0_dram": pack0(inputs),
              "shift_dram": shift, "state_dram": state}

    nc = bacc.Bacc("TRN2", target_bir_lowering=False, num_devices=1)
    aps = {n: nc.dram_tensor(n, v.shape, FP32, kind="ExternalInput").ap() for n, v in arrays.items()}
    out = nc.dram_tensor("out_dram", (PAIRS, P, C), FP32, kind="ExternalOutput").ap()
    build(nc, aps["x_dram"].rearrange("(a s) l n -> (s l) a n", s=2), aps["x_dram"], aps["ctx_dram"],
          aps["params_dram"], aps["params0_dram"], aps["shift_dram"], aps["state_dram"],
          out.rearrange("a p n -> p a n"))
    result = run_bass_kernel_spmd(nc, [arrays], core_ids=[0])
    return np.asarray(result.results[0]["out_dram"]).reshape(B, L, C)
```

```python
import numpy as np
import concourse.bass as bass
from concourse import mybir
from concourse.alu_op_type import AluOpType as ALU
from contextlib import ExitStack

FP32 = mybir.dt.float32
FR = mybir.dt.float32r
ACT = mybir.ActivationFunctionType

B, L, C = 32, 64, 256
P = 128
PAIRS = B // 2
CC = 64
HP = 4
QT = C // P
G = 8
GROUPS = B // G
GT = G * L
TT = GT // P
CT = C // P
HS = 8
MAA = 5
MD = 32
DD = 64
EPS = 1e-5

VECTORS = ["ln1_w", "ln1_b", "ln2_w", "ln2_b", "maa_x", "maa_w", "maa_k", "maa_v", "maa_r", "maa_g",
           "time_decay", "faaaa", "gn_w", "gn_b", "fmaa_k", "fmaa_r"]
SQUARES = ["Wr", "Wk", "Wv", "Wg", "Wo", "fWk", "fWr", "fWv"]

FIELDS0 = [("wqn", HP * P), ("wkn", HP * P), ("wvn", HP * P), ("bq", HP), ("wo", HP * CC), ("bv", HP),
           ("gamma", 1), ("beta", 1), ("bo", 1), ("mean64", P), ("pick", 2 * P), ("ident", P)]
FIELDS = [*[(n, CT) for n in VECTORS],
          ("maa_w1", CT * MAA * MD), ("maa_w2", C), ("maa_w2g", C), ("decay_w1", CT * DD), ("decay_w2", C),
          *[(n, CT * C) for n in SQUARES],
          ("ones8", P), ("mean8", P), ("centre8", P), ("spread", HS * P), ("gather", HS * P)]


def offsets(fields):
    at, out = 0, {}
    for name, width in fields:
        out[name] = (at, width)
        at += width
    return out, at


OFF, WIDTH = offsets(FIELDS)
OFF0, WIDTH0 = offsets(FIELDS0)


def build(nc, x, xs, ctxs, params, params0, shift, state, out):
    es = ExitStack()
    with es:
        def sb(name, shape):
            return es.enter_context(nc.sbuf_tensor(name, shape, FP32))

        def sem(name):
            return es.enter_context(nc.semaphore(name))

        params_sb = sb("params_sb", [P, WIDTH])

        def par(name, *dims):
            at, width = OFF[name]
            v = params_sb[:, at:at + width]
            if len(dims) == 2:
                v = v.rearrange("p (a b) -> p a b", a=dims[0])
            return v

        banks = [es.enter_context(nc.psum_tensor(f"bank{b}", [P, 512], FP32)) for b in range(8)]

        X = sb("X", [P, PAIRS, C])
        shift_sb = sb("shift_sb", [P, 2, CT, B])
        state_sb = sb("state_sb", [P, CT, HS, B])
        eps = sb("eps", [P, 1])

        ident = sb("ident", [P, P])[:, :]
        time_norm = Norm(sb, sem, "time")

        layer0(nc, sem, ident, banks, X, shift_sb, state_sb, eps, time_norm, params_sb, x, xs, ctxs, params, params0,
               shift, state)
        layer1(nc, sem, par, ident, banks, X, shift_sb, state_sb, eps, time_norm, out)


class Norm:
    def __init__(self, sb, sem, name):
        self.stat = sb("stat_" + name, [P, TT, 6])
        self.mom = sb("mom_" + name, [P, TT, 2])
        self.rstd = sb("rstd_" + name, [P, TT])
        self.xh = sb("xh_" + name, [P, TT, C])
        self.xa = sb("xa_" + name, [P, CT, G, L + 1])
        self.sx = sb("sx_" + name, [P, CT, GT])
        self.stats_done = sem("l1_stats_" + name)
        self.moments_done = sem("l1_moments_" + name)
        self.log_done = sem("l1_log_" + name)
        self.rstd_done = sem("l1_rstd_" + name)
        self.normalised = sem("l1_normalised_" + name)
        self.turned = sem("l1_turned_" + name)
        self.affine_done = sem("l1_affine_" + name)
        self.state_in = sem("l1_state_in_" + name)
        self.diff_done = sem("l1_diff_" + name)
        self.went = sem("l1_went_" + name)

    def moments(self, nc, dve, i, tile):
        for j in range(TT):
            nc.vector.bn_stats(self.stat[:, j, :], tile(j)).then_inc(self.stats_done, 1)
        dve.wait_ge(self.stats_done, TT * i + TT)
        dve.sem_inc(self.went, 1)
        for j in range(TT):
            nc.vector.bn_aggr(self.mom[:, j, :], self.stat[:, j, :]).then_inc(self.moments_done, 1)

    def normalise(self, nc, dve, i, tile):
        dve.wait_ge(self.rstd_done, i + 1)
        for j in range(TT):
            nc.vector.tensor_scalar(self.xh[:, j, :], tile(j), self.mom[:, j, 0:1], self.rstd[:, j:j + 1],
                                    ALU.subtract, ALU.mult).then_inc(self.normalised, 1)

    def log_var(self, nc, act, i, eps):
        act.wait_ge(self.moments_done, TT * i + TT)
        nc.scalar.activation(self.rstd[:, :], self.mom[:, :, 1], ACT.Ln, bias=eps[:, 0:1]).then_inc(self.log_done, 1)

    def inverse_std(self, nc, act, i):
        act.wait_ge(self.log_done, i + 1)
        nc.scalar.activation(self.rstd[:, :], self.rstd[:, :], ACT.Exp, scale=-0.5).then_inc(self.rstd_done, 1)


def token_tile(X, i):
    return lambda j: X[:, bass.ds(i * TT + j, 1), :].rearrange("p a n -> p (a n)")


def buffers(build_layer):
    def run(nc, *args):
        with ExitStack() as es:
            build_layer(nc, lambda name, shape, dtype=FP32: es.enter_context(nc.sbuf_tensor(name, shape, dtype)),
                        *args)
    return run


@buffers
def layer0(nc, sb, sem, ident, banks, X, shift_sb, state_sb, eps, N1, params_sb, x, xs, ctxs, params, params0, shift,
           state):
    p0 = sb("params0_sb", [P, WIDTH0])

    def par0(name, *dims):
        at, width = OFF0[name]
        t = p0[:, at:at + width]
        return t.rearrange("p (a b) -> p a b", a=dims[0]) if dims else t

    wqn, wkn, wvn = (par0(n, HP, P) for n in ("wqn", "wkn", "wvn"))
    wo = par0("wo", HP, CC)
    bq, bv, pick = par0("bq"), par0("bv"), par0("pick", 2, P)
    H = 2 * HP
    SCALE = CC ** -0.5

    stats = sb("stats", [P, PAIRS, 6])
    moments = sb("moments", [P, PAIRS, 2])
    offset = sb("offset", [P, PAIRS])
    spread = sb("spread_sq", [P, PAIRS])
    rstd = sb("gn_rstd_sb", [P, B])
    gn_scale = sb("gn_scale", [P, B])
    gn_shift = sb("gn_shift", [P, B])
    shift_neg = sb("shift_neg", [P, B])
    out_bias = sb("out_bias", [P, 1])
    wqk = sb("wqk", [P, H, P], FR)
    qq_bias = sb("qq_bias", [P, H])
    wz = sb("wz", [P, H, CC], FR)
    xd = [sb(f"xd{s}", [P, C]) for s in range(2)]
    cd = [sb(f"cd{s}", [P, C]) for s in range(2)]
    xn = sb("xn", [P, C])
    x1 = [sb(f"x1_{s}", [P, C], FR) for s in range(2)]
    x2 = [sb(f"x2_{s}", [P, C], FR) for s in range(2)]
    c1 = [sb(f"c1_{s}", [P, C], FR) for s in range(2)]
    c2 = [sb(f"c2_{s}", [P, C], FR) for s in range(2)]
    qq = sb("qq", [P, 4, 2, C], FR)
    z = [sb(f"z{s}", [P, QT, H * CC]) for s in range(2)]
    probs = sb("probs", [P, 2, 2, QT, C])
    neg_max = sb("neg_max", [P, 2, 4])
    sums = sb("sums", [P, 2, 4])
    recip = sb("recip", [P, 2, 4])
    pT = sb("pT", [P, 2, QT, C])
    o = sb("o", [P, QT, P])

    scores = [[banks[0], banks[1]], [banks[2], banks[3]]]
    turned = banks[4]
    acc = [banks[5][:, s * P:(s + 1) * P].rearrange("p (q c) -> p q c", q=QT) for s in range(2)]
    misc = [banks[6], banks[7]]
    out_T = misc[0][:, 0:C]

    def heads(bank):
        return bank[:, :].rearrange("p (h n) -> p h n", h=HP)

    def z_half(parity):
        return banks[4 + parity][:, 0:HP * CC].rearrange("p (h c) -> p h c", h=HP)

    loaded = [sem(f"loaded{q}") for q in range(4)]
    loaded_params0 = sem("loaded_params0")
    loaded_params = sem("loaded_params")
    state_loaded = sem("state_loaded")
    sample_loaded = [sem("sample_loaded0"), sem("sample_loaded1")]
    stats_done = sem("stats_done")
    gn_means = sem("gn_means")
    gn_offsets = sem("gn_offsets")
    gn_vars = sem("gn_vars")
    gn_log = sem("gn_log")
    gn_rstd = sem("gn_rstd")
    gn_affine = sem("gn_affine")
    eps_set = sem("eps_set")
    ident_copied = sem("ident_copied")
    folded = sem("folded")
    hi_split = sem("hi_split")
    split = sem("split")
    weights_ready = sem("weights_ready")
    xn_ready = sem("xn_ready")
    rounded = sem("rounded")
    prepared = sem("prepared")
    x_hi = sem("x_hi")
    x_parts = sem("x_parts")
    scores_ready = sem("scores_ready")
    max_ready = sem("max_ready")
    probs_ready = sem("probs_ready")
    recip_ready = sem("recip_ready")
    norm_ready = sem("norm_ready")
    turned_ready = sem("turned_ready")
    pT_ready = sem("pT_ready")
    pool_went = sem("pool_went")
    qq_full = sem("qq_full")
    qq_hi = sem("qq_hi")
    qq_ready = sem("qq_ready")
    z_full = sem("z_full")
    z_ready = sem("z_ready")
    acc_ready = sem("acc_ready")
    o_ready = sem("o_ready")
    out_ready = sem("out_ready")
    residual_added = sem("residual_added")

    TURN = {("qq", 0): 0, ("z", 0): 1, ("qq", 1): 2, ("qq", 2): 3, ("z", 1): 4, ("qq", 3): 5}

    def bank_of(item):
        return misc[TURN[item] % 2]

    U = HP
    LAST = U * B

    with nc.Block() as block:
        @block.sync
        def _(sp):
            for q in range(4):
                sl = slice(q * PAIRS // 4, (q + 1) * PAIRS // 4)
                sp.dma_start(X[:, sl, :], x[:, sl, :]).then_inc(loaded[q], 16)

            def load(n, par):
                for half in range(2):
                    rows = slice(CC * half, CC * half + CC)
                    sp.dma_start(xd[par][rows, :], xs[bass.ds(n, 1), :, :]).then_inc(sample_loaded[par], 16)
                    sp.dma_start(cd[par][rows, :], ctxs[bass.ds(n, 1), :, :]).then_inc(sample_loaded[par], 16)

            load(0, 0)
            load(1, 1)
            sp.dma_start(params_sb[:, :], params).then_inc(loaded_params, 16)
            sp.dma_start(shift_sb[:, :, :, :], shift).then_inc(state_loaded, 16)
            sp.dma_start(state_sb[:, :, :, :], state).then_inc(state_loaded, 16)
            with sp.Fori(0, PAIRS - 1) as i:
                for par in range(2):
                    sp.wait_ge(prepared, 2 * i + (par + 1))
                    sp.wait_ge(xn_ready, 2 * i + (par + 1))
                    load(2 * i + par + 2, par)
            sp.wait_ge(loaded_params, 16)
            sp.wait_ge(state_loaded, 32)

        @block.gpsimd
        def _(pool):
            def wait_apart(semaphore, value):
                pool.wait_ge(semaphore, value)
                pool.sem_inc(pool_went, 1)

            def prepare(n, par, loads):
                wait_apart(sample_loaded[par], 64 * loads)
                nc.gpsimd.tensor_scalar(c1[par][:, :], cd[par][:, :], 1.0, 0.0, ALU.mult, ALU.add)\
                    .then_inc(rounded, 1)
                pool.wait_ge(rounded, n + 1)
                nc.gpsimd.tensor_tensor(c2[par][:, :], cd[par][:, :], c1[par][:, :].bitcast(FP32), ALU.subtract)\
                    .then_inc(prepared, 1)
                wait_apart(xn_ready, n + 1)
                nc.gpsimd.tensor_scalar(x1[par][:, :], xn[:, :], 1.0, 0.0, ALU.mult, ALU.add).then_inc(x_hi, 1)

            def normalise(g, u):
                s = u % 2
                wait_apart(recip_ready, g + 1)
                for h in range(2):
                    for q in range(QT):
                        n = 2 * h + q
                        row = probs[:, s, h, q, :]
                        nc.gpsimd.tensor_scalar(row, row, recip[:, s, n:n + 1], 1.0, ALU.mult, ALU.mult)\
                            .then_inc(norm_ready, 1)

            prepare(0, 0, 1)
            prepare(1, 1, 1)
            normalise(0, 0)

            def body(i, last):
                for s in range(2):
                    for v in range(U):
                        g = 2 * U * i + (U * s + v)
                        if not last or U * s + v + 1 < 2 * U:
                            normalise(g + 1, v + 1)
                        if v == 2 and not last:
                            prepare(2 * i + (s + 2), s, i + 2)

            with pool.Fori(0, PAIRS - 1) as i:
                body(i, False)
            body(PAIRS - 1, True)

        @block.vector
        def _(dve):
            def shape3(bank):
                return bank[:, :].rearrange("p (a n) -> p a n", a=2)

            dve.sem_inc(pT_ready, 1)
            dve.wait_ge(loaded_params0, 16)
            nc.vector.tensor_copy(ident[:, :], par0("ident")).then_inc(ident_copied, 1)
            nc.vector.memset(eps[:, :], EPS).then_inc(eps_set, 1)
            for p in range(PAIRS):
                if p % (PAIRS // 4) == 0:
                    dve.wait_ge(loaded[p // (PAIRS // 4)], 16)
                nc.vector.bn_stats(stats[:, p, :], X[:, p, :]).then_inc(stats_done, 1)
            for p in range(PAIRS):
                dve.wait_ge(stats_done, p + 1)
                nc.vector.bn_aggr(moments[:, p, :], stats[:, p, :]).then_inc(stats_done, 1)
            mean, var = moments[:, :, 0], moments[:, :, 1]
            dve.wait_ge(stats_done, 2 * PAIRS)
            dve.wait_ge(gn_means, 1)
            nc.vector.tensor_tensor(offset[:, :], mean, misc[0][:, 0:PAIRS], ALU.subtract).then_inc(gn_offsets, 1)
            dve.wait_ge(gn_offsets, 1)
            nc.vector.tensor_tensor(spread[:, :], offset[:, :], offset[:, :], ALU.mult).then_inc(gn_offsets, 1)
            dve.wait_ge(gn_offsets, 2)
            nc.vector.tensor_tensor(spread[:, :], spread[:, :], var, ALU.add).then_inc(gn_offsets, 1)
            dve.wait_ge(gn_rstd, 1)
            nc.vector.tensor_scalar(gn_scale[:, :], rstd[:, :], par0("gamma"), None, ALU.mult).then_inc(gn_affine, 1)
            dve.wait_ge(gn_affine, 1)
            nc.vector.tensor_tensor(shift_neg[:, :], gn_scale[:, :], misc[0][:, B:2 * B], ALU.mult)\
                .then_inc(gn_affine, 1)
            dve.wait_ge(gn_affine, 2)
            nc.vector.tensor_scalar(gn_shift[:, :], shift_neg[:, :], -1.0, par0("beta"), ALU.mult, ALU.add)\
                .then_inc(gn_affine, 1)
            dve.wait_ge(gn_affine, 3)

            def affine(n, par, loads):
                dve.wait_ge(sample_loaded[par], 64 * loads)
                nc.vector.tensor_scalar(xn[:, :], xd[par][:, :], gn_scale[:, bass.ds(n, 1)],
                                        gn_shift[:, bass.ds(n, 1)], ALU.mult, ALU.add).then_inc(xn_ready, 1)

            def lower_part(n, par):
                dve.wait_ge(x_hi, n + 1)
                nc.vector.tensor_tensor(x2[par][:, :], xn[:, :], x1[par][:, :].bitcast(FP32), ALU.subtract)\
                    .then_inc(x_parts, 1)
                dve.wait_ge(x_parts, n + 1)

            affine(0, 0, 1)
            lower_part(0, 0)
            affine(1, 1, 1)
            for b in range(2):
                dve.wait_ge(hi_split, 2 * (b + 1))
                nc.vector.scalar_tensor_tensor(wqk[CC:P, b::2, :], heads(banks[b])[CC:P], SCALE,
                                               wqk[CC:P, b::2, :].bitcast(FP32), ALU.mult, ALU.subtract)\
                    .then_inc(split, 1)
                nc.vector.tensor_scalar(qq_bias[:, b::2], banks[2 + b][:, 0:HP], SCALE, None, ALU.mult)\
                    .then_inc(split, 1)
                nc.vector.tensor_tensor(wz[CC:P, b::2, :], z_half(b)[CC:P], wz[CC:P, b::2, :].bitcast(FP32),
                                        ALU.subtract).then_inc(split, 1)
            nc.vector.tensor_tensor(out_bias[:, :], par0("bo"), banks[7][:, 0:1], ALU.add).then_inc(split, 1)
            dve.wait_ge(split, 7)
            dve.sem_inc(weights_ready, 1)

            def row_max(g, u):
                s = u % 2
                dve.wait_ge(scores_ready, g + 1)
                for h in range(2):
                    ins = nc.vector.tensor_reduce(neg_max[:, s, 2 * h:2 * h + 2], shape3(scores[s][h]),
                                                  mybir.AxisListType.X, ALU.max, negate=True)
                ins.then_inc(max_ready, 1)

            def invert_sums(g, u):
                s = u % 2
                dve.wait_ge(probs_ready, 4 * g + 4)
                nc.vector.reciprocal(recip[:, s, :], sums[:, s, :]).then_inc(recip_ready, 1)

            def copy_pT(g, h):
                dve.wait_ge(turned_ready, 2 * g + (h + 1))
                nc.vector.tensor_copy(pT[:, h, :, :], shape3(turned)).then_inc(pT_ready, 1)

            def take_lo(n, v):
                dve.wait_ge(qq_hi, U * n + (v + 1))
                bank = bank_of(("qq", v))
                for h in range(2):
                    slot = qq[CC:P, v, h, :]
                    ins = nc.vector.scalar_tensor_tensor(slot, shape3(bank)[CC:P, h, :],
                                                         qq_bias[CC:P, 2 * v + h:2 * v + h + 1], slot.bitcast(FP32),
                                                         ALU.add, ALU.subtract)
                ins.then_inc(qq_ready, 1)

            take_lo(0, 0)
            take_lo(0, 1)
            row_max(0, 0)
            take_lo(0, 2)
            row_max(1, 1)
            lower_part(1, 1)
            invert_sums(0, 0)
            take_lo(0, 3)

            def take_output(m, s):
                dve.wait_ge(acc_ready, m + 1)
                nc.vector.tensor_copy(o[:, :, s * CC:(s + 1) * CC], acc[s]).then_inc(o_ready, 1)

            def add_residual(i):
                dve.wait_ge(out_ready, i + 1)
                xi = X[:, bass.ds(i, 1), :].rearrange("p a n -> p (a n)")
                nc.vector.scalar_tensor_tensor(xi, out_T, out_bias[:, 0:1], xi, ALU.add, ALU.add)\
                    .then_inc(residual_added, 1)

            def body(i, first, last):
                for s in range(2):
                    m = 2 * i + s
                    for v in range(U):
                        g = 2 * U * i + (U * s + v)
                        left = 2 * U - (U * s + v) if last else 2 * U
                        if s == 1 and v == 0 and not first:
                            add_residual(i - 1)
                        copy_pT(g, 0)
                        if left > 1:
                            invert_sums(g + 1, v + 1)
                        if v == 0 and not (first and s == 0):
                            take_output(m - 1, 1 - s)
                        if left > 2:
                            row_max(g + 2, v)
                        copy_pT(g, 1)
                        if not (last and s == 1):
                            take_lo(m + 1, v)
                        if last and s == 1 and v == 2:
                            N1.moments(nc, dve, 0, token_tile(X, 0))
                        if last and s == 1 and v == 3:
                            N1.normalise(nc, dve, 0, token_tile(X, 0))
                        if v == 2 and not last:
                            affine(m + 2, s, i + 2)
                        if v == 3 and not last:
                            lower_part(m + 2, s)

            body(0, True, False)
            with dve.Fori(1, PAIRS - 1) as i:
                body(i, False, False)
            body(PAIRS - 1, False, True)
            take_output(B - 1, 1)
            add_residual(PAIRS - 1)

        @block.scalar
        def _(act):
            act.dma_start(p0[:, :], params0).then_inc(loaded_params0, 16)
            act.wait_ge(eps_set, 1)
            act.wait_ge(gn_vars, 1)
            nc.scalar.activation(rstd[:, :], misc[0][:, 2 * B:3 * B], ACT.Ln, bias=eps[:, 0:1]).then_inc(gn_log, 1)
            act.wait_ge(gn_log, 1)
            nc.scalar.activation(rstd[:, :], rstd[:, :], ACT.Exp, scale=-0.5).then_inc(gn_rstd, 1)
            act.wait_ge(folded, 1)
            for b in range(2):
                nc.scalar.activation(wqk[:, b::2, :], heads(banks[b]), ACT.Copy, scale=SCALE).then_inc(hi_split, 1)
                nc.scalar.copy(wz[:, b::2, :], z_half(b)).then_inc(hi_split, 1)

            def exps(g, u):
                s = u % 2
                act.wait_ge(max_ready, g + 1)
                for h in range(2):
                    if h == 1 and not isinstance(g, int) or h == 1 and g >= 2:
                        act.wait_ge(turned_ready, 2 * (g - 1))
                    for q in range(QT):
                        n = 2 * h + q
                        nc.scalar.activation(probs[:, s, h, q, :], scores[s][h][:, q * C:(q + 1) * C], ACT.Exp,
                                             bias=neg_max[:, s, n:n + 1], accum_out=sums[:, s, n:n + 1])\
                            .then_inc(probs_ready, 1)

            def take(n, par, item):
                kind, v = item
                bank = bank_of(item)
                if kind == "qq":
                    act.wait_ge(qq_full, U * n + (v + 1))
                    for h in range(2):
                        ins = nc.scalar.activation(qq[:, v, h, :], bank[:, h * C:(h + 1) * C], ACT.Identity,
                                                   bias=qq_bias[:, 2 * v + h:2 * v + h + 1])
                    ins.then_inc(qq_hi, 1)
                else:
                    act.wait_ge(z_full, QT * n + (v + 1))
                    nc.scalar.copy(z[par][:, v, :], bank[:, :]).then_inc(z_ready, 1)

            for item in (("qq", 0), ("z", 0), ("qq", 1), ("qq", 2)):
                take(0, 0, item)
            exps(0, 0)
            take(0, 0, ("z", 1))
            exps(1, 1)
            take(0, 0, ("qq", 3))

            def body(i, last):
                for s in range(2):
                    for v in range(U):
                        g = 2 * U * i + (U * s + v)
                        more = not (last and s == 1)
                        if more:
                            take(2 * i + (s + 1), 1 - s, ("qq", v))
                        if not last or U * s + v + 2 < 2 * U:
                            exps(g + 2, v)
                        if more and v in (0, 2):
                            take(2 * i + (s + 1), 1 - s, ("z", v // 2))

            with act.Fori(0, PAIRS - 1) as i:
                body(i, False)
            body(PAIRS - 1, True)
            N1.log_var(nc, act, 0, eps)
            N1.inverse_std(nc, act, 0)

        @block.tensor
        def _(pe):
            pe.wait_ge(loaded_params0, 16)
            by_sample = [misc[0][:, (1 + k) * B:(2 + k) * B].rearrange("p (i s) -> p i s", s=2) for k in range(2)]
            for h in range(H):
                if h == 5:
                    pe.wait_ge(stats_done, 2 * PAIRS)
                    nc.tensor.matmul(misc[0][:, 0:PAIRS], par0("mean64"), moments[:, :, 0], start=True, stop=True)
                    for s in range(2):
                        ins = nc.tensor.matmul(by_sample[0][:, :, s], pick[:, s, :], moments[:, :, 0],
                                               start=True, stop=True)
                    ins.then_inc(gn_means, 1)
                if h == 7:
                    pe.wait_ge(gn_offsets, 3)
                    for s in range(2):
                        ins = nc.tensor.matmul(by_sample[1][:, :, s], pick[:, s, :], spread[:, :],
                                               start=True, stop=True)
                    ins.then_inc(gn_vars, 1)
                hp, rows = h // 2, slice(CC * (h % 2), CC * (h % 2) + CC)
                cols = slice(hp * P, hp * P + P)
                nc.tensor.matmul(banks[h % 2][:, cols], wqn[rows, hp, :], wkn[rows, hp, :], start=True, stop=True)
                nc.tensor.matmul(banks[2 + h % 2][:, hp:hp + 1], wkn[rows, hp, :], bq[rows, hp:hp + 1],
                                 start=True, stop=True)
                nc.tensor.matmul(z_half(h % 2)[:, hp, :], wvn[rows, hp, :], wo[rows, hp, :],
                                 start=True, stop=True)
            for smp in range(2):
                for hp in range(HP):
                    ins = nc.tensor.matmul(banks[7][CC * smp:CC * smp + CC, 0:1], wo[:, hp, :], bv[:, hp:hp + 1],
                                           start=hp == 0, stop=hp == HP - 1)
            ins.then_inc(folded, 1)
            def product(n, par, item):
                kind, v = item
                bank = bank_of(item)
                first = isinstance(n, int) and n == 0
                if item == ("qq", 0) and not first:
                    pe.wait_ge(z_ready, QT * (n - 1) + 2)
                if item == ("z", 0) and not first:
                    pe.wait_ge(qq_ready, U * (n - 1) + 4)
                if item == ("qq", 1):
                    pe.wait_ge(qq_ready, U * n + 1)
                if item == ("qq", 2):
                    pe.wait_ge(z_ready, QT * n + 1)
                if item == ("z", 1):
                    pe.wait_ge(qq_ready, U * n + 2)
                if item == ("qq", 3):
                    pe.wait_ge(qq_ready, U * n + 3)
                if v == 0:
                    pe.wait_ge(prepared, n + 1)
                    pe.wait_ge(x_parts, n + 1)
                if kind == "qq":
                    for h in range(2):
                        out = bank[:, h * C:(h + 1) * C]
                        nc.tensor.matmul(out, wqk[:, 2 * v + h, :], x1[par][:, :], start=True, stop=False)
                        ins = nc.tensor.matmul(out, wqk[:, 2 * v + h, :], x2[par][:, :], start=False, stop=True)
                    ins.then_inc(qq_full, 1)
                else:
                    cols = slice(v * P, (v + 1) * P)
                    nc.tensor.matmul(bank[:, :], c1[par][:, cols], wz[:, :, :], start=True, stop=False)
                    nc.tensor.matmul(bank[:, :], c2[par][:, cols], wz[:, :, :], start=False, stop=True)\
                        .then_inc(z_full, 1)

            def score(g, par, v):
                pe.wait_ge(qq_ready, g + 1)
                if not isinstance(g, int) or g >= 2:
                    pe.wait_ge(probs_ready, 4 * (g - 1))
                for h in range(2):
                    for q in range(QT):
                        out = scores[v % 2][h][:, q * C:(q + 1) * C]
                        w = qq[:, v, h, q * P:(q + 1) * P]
                        nc.tensor.matmul(out, w, c1[par][:, :], start=True, stop=False)
                        ins = nc.tensor.matmul(out, w, c2[par][:, :], start=False, stop=True)
                ins.then_inc(scores_ready, 1)

            def turn(g, v, h):
                pe.wait_ge(norm_ready, 4 * g + (2 * h + 2))
                pe.wait_ge(pT_ready, 2 * g + (h + 1))
                for k in range(QT):
                    for q in range(QT):
                        ins = nc.tensor.transpose(turned[:, k * C + q * P:k * C + q * P + P],
                                                  probs[:, v % 2, h, q, k * P:(k + 1) * P], ident)
                ins.then_inc(turned_ready, 1)

            def attend(g, s, v, h):
                pe.wait_ge(pT_ready, 2 * g + (h + 2))
                for k in range(QT):
                    for q in range(QT):
                        head = 2 * v + h
                        ins = nc.tensor.matmul(acc[s][:, q, :], pT[:, h, k, q * P:(q + 1) * P],
                                               z[s][:, k, head * CC:(head + 1) * CC],
                                               start=head == 0 and k == 0 and q == 0,
                                               stop=head == H - 1 and k == QT - 1, skip_group_check=True)
                return ins

            pe.wait_ge(weights_ready, 1)
            pe.wait_ge(ident_copied, 1)
            for item in (("qq", 0), ("z", 0), ("qq", 1)):
                product(0, 0, item)
            score(0, 0, 0)
            product(0, 0, ("qq", 2))
            score(1, 0, 1)
            product(0, 0, ("z", 1))
            product(0, 0, ("qq", 3))

            def body(i, first, last):
                for s in range(2):
                    m = 2 * i + s
                    for v in range(U):
                        g = 2 * U * i + (U * s + v)
                        start, more = first and s == 0 and v == 0, not (last and s == 1)
                        turn(g, v, 0)
                        if not last or U * s + v + 2 < 2 * U:
                            score(g + 2, s if v < 2 else 1 - s, (v + 2) % U)
                        if not start:
                            ins = attend(g - 1, s if v else 1 - s, (v - 1) % U, 1)
                            if v == 0:
                                ins.then_inc(acc_ready, 1)
                        if more:
                            if s == 1 and v == 0 and not first:
                                pe.wait_ge(residual_added, i)
                            product(m + 1, 1 - s, ("qq", v))
                        turn(g, v, 1)
                        if v == 0:
                            pe.wait_ge(z_ready, 2 * QT * i + QT * (s + 1))
                            if not start:
                                pe.wait_ge(o_ready, m)
                        attend(g, s, v, 0)
                        if more and v in (0, 2):
                            product(m + 1, 1 - s, ("z", v // 2))
                        if s == 0 and v == U - 1 and not first:
                            pe.wait_ge(z_ready, QT * (2 * i + 2))
                            turn_out(i - 1)

            def turn_out(i):
                pe.wait_ge(o_ready, 2 * i + 2)
                for q in range(QT):
                    ins = nc.tensor.transpose(out_T[:, q * P:(q + 1) * P], o[:, q, :], ident)
                ins.then_inc(out_ready, 1)

            body(0, True, False)
            with pe.Fori(1, PAIRS - 1) as i:
                body(i, False, False)
            body(PAIRS - 1, False, True)
            attend(LAST - 1, 1, U - 1, 1).then_inc(acc_ready, 1)
            turn_out(PAIRS - 1)


@buffers
def layer1(nc, sb, sem, par, ident, banks, X, shift_sb, state_sb, eps, N1, out):
    ones8, mean8, centre8 = par("ones8"), par("mean8"), par("centre8")
    gather = par("gather", HS, P)
    maa_w1, maa_w2, maa_w2g = par("maa_w1", CT, MAA * MD), par("maa_w2"), par("maa_w2g")
    decay_w1, decay_w2 = par("decay_w1", CT, DD), par("decay_w2")
    W = {n: par(n, CT, C) for n in SQUARES}
    vec = {n: par(n) for n in VECTORS}

    N2 = Norm(sb, sem, "channel")
    low1 = sb("low1", [P, GT])
    low2 = sb("low2", [MD, GT])
    xj = [sb(f"xj{j}", [P, CT, GT]) for j in range(MAA)]
    dh = sb("dh", [DD, GT])
    we = sb("we", [P, CT, GT])
    wd = sb("wd", [P, CT, G, L])
    r = sb("r", [P, CT, GT])
    k = sb("k", [P, CT, GT])
    v1 = sb("v1", [P, CT, GT])
    vhi = sb("vhi", [P, CT, GT], FR)
    vlo = sb("vlo", [P, CT, GT], FR)
    spread = sb("spread_fr", [P, HS, P], FR)
    g = sb("g", [P, CT, GT])
    qv = sb("qv", [P, CT, GT])
    RING = 4
    VRING = 2
    a = sb("a", [P, RING, G, L])
    s = sb("s", [P, RING, GT])
    rs = sb("rs", [P, RING, GT])
    yc = sb("yc", [P, CT, GT])
    yd = sb("yd", [P, CT, GT])
    sq = sb("sq", [P, CT, GT])
    xx = sq
    fx = [sb(f"fx{n}", [P, CT, GT]) for n in range(2)]
    kk = sb("kk", [P, CT, GT])
    rr = sb("rr", [P, CT, GT])

    names = ["constants_rounded", "low_input", "low_product", "low_tanh", "mix_product", "mix_difference",
             "input_mixed", "projected", "projection_taken", "decay_ready", "gate_product", "gate_sigmoid",
             "gate_ready", "v_high", "v_low", "v_spread", "first_state_in", "kv_ready", "state_ready", "rs_ready",
             "rs_summed", "ruk_ready", "ruk_summed", "own_part_ready", "heads_out", "centred", "squared", "group_var",
             "group_log", "group_rstd", "scaled", "group_affine", "gated", "output_product", "residual_added",
             "key_input", "receptance_input", "key_product", "key_relu", "key_squared", "receptance_product",
             "receptance_sigmoid", "value_product", "value_gated", "output_ready", "stored"]
    S = {n: sem("l1_" + n) for n in names}

    y_banks = banks[0:2]
    proj_banks = banks[2:6]
    mix_banks = banks[2:4]
    v_banks = [banks[5], banks[4]]
    c_banks = banks[6:8]
    gate_bank = banks[1]
    GATE_STEPS = (0, 3)

    def grouped(t):
        return t.rearrange("p (b l) -> p b l", b=G)

    def token_tiles(bank):
        return bank.rearrange("p (a n) -> p a n", a=2)

    PROJ = [("dec1", 0), ("k", 0), ("k", 1), ("dec2", 0), ("dec2", 1), ("r", 0), ("r", 1), ("v", 0), ("v", 1),
            ("q", 0), ("q", 1)]
    AT = {item: n for n, item in enumerate(PROJ)}
    NP = AT["q", 0]
    MIX = [(j, c) for j in (0, 1, 3, 2, 4) for c in range(CT)]
    MIX_ORDER = [j for j, c in MIX if c == 1]
    NM = len(MIX)
    SRC = {"dec1": 0, "k": 1, "v": 2, "r": 3, "g": 4}
    MAA_NAMES = ["maa_w", "maa_k", "maa_v", "maa_r", "maa_g"]
    STEPS = [(c, t) for c in range(CT) for t in range(HS)]
    NS = len(STEPS)

    def schedule(engine, between, during):
        during(-2, False, False, True)
        between(-1, True, False, True)
        during(-1, True, False, True)
        with engine.Fori(0, GROUPS - 2) as i:
            between(i, True, True, True)
            during(i, True, True, True)
        between(GROUPS - 2, True, True, False)
        during(GROUPS - 2, True, True, False)
        between(GROUPS - 1, False, True, False)
        during(GROUPS - 1, False, True, False)

    with nc.Block() as block:
        @block.sync
        def _(sp):
            with sp.Fori(0, GROUPS) as i:
                for b in range(2):
                    sp.wait_ge(S["output_ready"], 2 * i + (b + 1))
                    half = bass.ds(i * TT + 2 * b, 2)
                    sp.dma_start(out[:, half, :], X[:, half, :]).then_inc(S["stored"], 16)
            sp.wait_ge(S["stored"], 2 * 16 * GROUPS)

        @block.gpsimd
        def _(pool):
            nc.gpsimd.memset(wd[:, :, :, 0:1], 0.0)

            def state_in(N, i, which):
                for c in range(CT):
                    nc.gpsimd.tensor_copy(N.xa[:, c, :, 0], shift_sb[:, which, c, bass.ds(i * G, G)])\
                        .then_inc(N.state_in, 1)

            def diff(N, i, c):
                pool.wait_ge(N.affine_done, CT * i + c + 1)
                pool.wait_ge(N.state_in, CT * i + c + 1)
                nc.gpsimd.tensor_tensor(grouped(N.sx[:, c, :]), N.xa[:, c, :, 0:L], N.xa[:, c, :, 1:L + 1],
                                        ALU.subtract).then_inc(N.diff_done, 1)

            def first_state(i, n):
                c, t = STEPS[n]
                nc.gpsimd.tensor_copy(a[:, n % RING, :, 0], state_sb[:, c, t, bass.ds(i * G, G)])\
                    .then_inc(S["first_state_in"], 1)

            def weigh(i, n):
                c, t = STEPS[n]
                m = n % RING
                pool.wait_ge(S["state_ready"], NS * i + n + 1)
                if n + RING < NS:
                    first_state(i, n + RING)
                if n >= RING:
                    pool.wait_ge(S["rs_summed"], NS * i + (n - RING + 1))
                nc.gpsimd.tensor_tensor(rs[:, m, :], r[:, c, :], s[:, m, :], ALU.mult).then_inc(S["rs_ready"], 1)

            def add_input(i, n):
                j, c = MIX[n]
                pool.wait_ge(S["mix_difference"], NM * i + n + 1)
                nc.gpsimd.tensor_tensor(grouped(xj[j][:, c, :]), grouped(xj[j][:, c, :]), N1.xa[:, c, :, 1:L + 1],
                                        ALU.add).then_inc(S["input_mixed"], 1)

            def add_output(i, b):
                pool.wait_ge(S["value_gated"], 2 * i + b + 1)
                xb = X[:, bass.ds(i * TT + 2 * b, 2), :]
                nc.gpsimd.tensor_tensor(xb, token_tiles(rr[:, b, :]), xb, ALU.add).then_inc(S["output_ready"], 1)

            def between(i, project, c, norm):
                pass

            def during(i, recur, chan, mix):
                if recur:
                    for n in range(RING):
                        first_state(i + 1, n)
                if mix:
                    state_in(N1, i + 2, 1)
                if chan:
                    state_in(N2, i, 0)
                for n in range(NS):
                    if recur:
                        weigh(i + 1, n)
                    if mix and n < CT:
                        diff(N1, i + 2, n)
                    if chan and n in (3, 4):
                        diff(N2, i, n - 3)
                    if mix and 0 <= n - 8 < NM:
                        add_input(i + 2, n - 8)
                if mix:
                    for n in range(NS - 8, NM):
                        add_input(i + 2, n)
                if chan:
                    for b in range(2):
                        add_output(i, b)

            schedule(pool, between, during)

        @block.vector
        def _(dve):
            nc.vector.tensor_copy(spread[:, :, :], par("spread", HS, P)).then_inc(S["constants_rounded"], 1)

            def mixed(dst, N, weight, c, done):
                nc.vector.scalar_tensor_tensor(grouped(dst[:, c, :]), grouped(N.sx[:, c, :]),
                                               vec[weight][:, c:c + 1], N.xa[:, c, :, 1:L + 1],
                                               ALU.mult, ALU.add).then_inc(done, 1)

            def mix_difference(i, n):
                j, c = MIX[n]
                dve.wait_ge(S["mix_product"], NM * i + n + 1)
                nc.vector.scalar_tensor_tensor(xj[j][:, c, :], mix_banks[n % 2][:, :], vec[MAA_NAMES[j]][:, c:c + 1],
                                               N1.sx[:, c, :], ALU.add, ALU.mult).then_inc(S["mix_difference"], 1)

            def recur_step(i, n):
                c, t = STEPS[n]
                m = n % RING
                dve.wait_ge(S["v_spread"], NS * i + n + 1)
                nc.vector.tensor_tensor(a[:, m, :, 1:L], grouped(v_banks[n % VRING][:, :])[:, :, 0:L - 1],
                                        grouped(k[:, c, :])[:, :, 0:L - 1], ALU.mult).then_inc(S["kv_ready"], 1)
                dve.wait_ge(S["kv_ready"], NS * i + n + 1)
                dve.wait_ge(S["first_state_in"], NS * i + n + 1)
                if n >= RING:
                    dve.wait_ge(S["rs_ready"], NS * i + (n - RING + 1))
                nc.vector.tensor_tensor_scan(s[:, m, :], wd[:, c, :, :].rearrange("p b l -> p (b l)"),
                                             a[:, m, :, :].rearrange("p b l -> p (b l)"), 0.0,
                                             ALU.mult, ALU.add).then_inc(S["state_ready"], 1)

            def between(i, project, chan, norm):
                if chan:
                    for c in range(CT):
                        dve.wait_ge(S["rs_summed"], NS * i + (c + 1) * HS)
                        nc.vector.tensor_tensor(yc[:, c, :], y_banks[c][:, :], qv[:, c, :], ALU.add)\
                            .then_inc(S["heads_out"], 1)
                if norm:
                    N1.moments(nc, dve, i + 2, token_tile(X, i + 2))
                if chan:
                    for c in range(CT):
                        dve.wait_ge(S["group_rstd"], CT * i + c + 1)
                        nc.vector.tensor_tensor(yd[:, c, :], c_banks[c][:, :], yc[:, c, :], ALU.mult)\
                            .then_inc(S["scaled"], 1)
                    for c in range(CT):
                        dve.wait_ge(S["scaled"], CT * i + c + 1)
                        nc.vector.tensor_scalar(yd[:, c, :], yd[:, c, :], vec["gn_w"][:, c:c + 1],
                                                vec["gn_b"][:, c:c + 1], ALU.mult, ALU.add)\
                                                    .then_inc(S["group_affine"], 1)
                    for c in range(CT):
                        dve.wait_ge(S["group_affine"], CT * i + c + 1)
                        nc.vector.tensor_tensor(yc[:, c, :], yd[:, c, :], g[:, c, :], ALU.mult)\
                            .then_inc(S["gated"], 1)
                if norm:
                    N1.normalise(nc, dve, i + 2, token_tile(X, i + 2))
                if project:
                    for c in range(CT):
                        dve.wait_ge(S["projection_taken"], NP * (i + 1) + (AT["r", c] + 1))
                        nc.vector.scalar_tensor_tensor(qv[:, c, :], k[:, c, :], vec["faaaa"][:, c:c + 1], r[:, c, :],
                                                       ALU.mult, ALU.mult).then_inc(S["ruk_ready"], 1)
                    for c in range(CT):
                        dve.wait_ge(S["v_high"], CT * (i + 1) + c + 1)
                        nc.vector.tensor_tensor(vlo[:, c, :], v1[:, c, :], vhi[:, c, :].bitcast(FP32), ALU.subtract)\
                            .then_inc(S["v_low"], 1)
                    for c in range(CT):
                        dve.wait_ge(S["ruk_summed"], CT * (i + 1) + c + 1)
                        nc.vector.tensor_tensor(qv[:, c, :], proj_banks[AT["q", c] % 4][:, :], v1[:, c, :], ALU.mult)\
                            .then_inc(S["own_part_ready"], 1)
                if chan:
                    for b in range(2):
                        dve.wait_ge(S["output_product"], 2 * i + b + 1)
                        xb = X[:, bass.ds(i * TT + 2 * b, 2), :]
                        nc.vector.tensor_tensor(xb, token_tiles(c_banks[b][:, :]), xb, ALU.add)\
                            .then_inc(S["residual_added"], 1)
                    dve.wait_ge(S["residual_added"], 2 * (i + 1))
                    dve.sem_inc(N2.went, 1)
                    N2.moments(nc, dve, i, token_tile(X, i))

            def during(i, recur, chan, mix):
                if recur:
                    dve.wait_ge(S["decay_ready"], CT * (i + 2))
                for n in range(NS):
                    if chan and n == 1:
                        N2.normalise(nc, dve, i, token_tile(X, i))
                    if mix and n == 3:
                        for c in range(CT):
                            dve.wait_ge(N1.diff_done, CT * (i + 2) + c + 1)
                            mixed(xx, N1, "maa_x", c, S["low_input"])
                    if chan and n in (6, 7):
                        for c in range(CT):
                            dve.wait_ge(N2.diff_done, CT * i + c + 1)
                            mixed(fx[n - 6], N2, ("fmaa_k", "fmaa_r")[n - 6], c,
                                  S[("key_input", "receptance_input")[n - 6]])
                    if recur:
                        recur_step(i + 1, n)
                    if recur and n - 2 in GATE_STEPS:
                        c = GATE_STEPS.index(n - 2)
                        dve.wait_ge(S["gate_sigmoid"], CT * (i + 1) + c + 1)
                        nc.vector.tensor_tensor(g[:, c, :], gate_bank[:, :], g[:, c, :], ALU.mult)\
                            .then_inc(S["gate_ready"], 1)
                    if mix and 0 <= n - 7 < NM:
                        mix_difference(i + 2, n - 7)
                if mix:
                    mix_difference(i + 2, NM - 1)
                if chan:
                    for b in range(2):
                        dve.wait_ge(S["value_product"], 2 * i + b + 1)
                        dve.wait_ge(S["receptance_sigmoid"], 2 * i + b + 1)
                        nc.vector.tensor_tensor(rr[:, b, :], c_banks[b][:, :], rr[:, b, :], ALU.mult)\
                            .then_inc(S["value_gated"], 1)

            schedule(dve, between, during)

        @block.scalar
        def _(act):
            def affine(N, i, w, b, at):
                for c in range(CT):
                    act.wait_ge(N.turned, CT * i + c + 1)
                    nc.scalar.activation(N.xa[:, c, :, 1:L + 1], grouped(at[c][:, :]), ACT.Identity,
                                         scale=vec[w][:, c:c + 1], bias=vec[b][:, c:c + 1]).then_inc(N.affine_done, 1)

            def take(i, name, c):
                n = AT[name, c]
                act.wait_ge(S["projected"], NP * i + n + 1)
                bank = proj_banks[n % 4]
                if name == "dec1":
                    nc.scalar.activation(dh[:, :], bank[0:DD, :], ACT.Tanh).then_inc(S["projection_taken"], 1)
                elif name == "dec2":
                    nc.scalar.activation(we[:, c, :], bank[:, :], ACT.Exp, bias=vec["time_decay"][:, c:c + 1])\
                        .then_inc(S["projection_taken"], 1)
                    act.wait_ge(S["projection_taken"], NP * i + n + 1)
                    nc.scalar.activation(wd[:, c, :, 1:L], grouped(we[:, c, :])[:, :, 0:L - 1], ACT.Exp, scale=-1.0)\
                        .then_inc(S["decay_ready"], 1)
                else:
                    nc.scalar.copy({"k": k, "r": r, "v": v1}[name][:, c, :], bank[:, :])\
                        .then_inc(S["projection_taken"], 1)
                    if name == "v":
                        act.wait_ge(S["projection_taken"], NP * i + n + 1)
                        nc.scalar.copy(vhi[:, c, :], v1[:, c, :]).then_inc(S["v_high"], 1)

            def between(i, project, chan, norm):
                if project:
                    take(i + 1, "dec1", 0)
                    if chan:
                        act.wait_ge(S["rs_ready"], NS * (i + 1))
                    take(i + 1, "k", 0)
                    take(i + 1, "k", 1)
                if chan:
                    for c in range(CT):
                        act.wait_ge(S["centred"], CT * i + c + 1)
                        nc.scalar.activation(sq[:, c, :], c_banks[c][:, :], ACT.Square).then_inc(S["squared"], 1)
                    for c in range(CT):
                        act.wait_ge(S["group_var"], CT * i + c + 1)
                        nc.scalar.activation(sq[:, c, :], y_banks[c][:, :], ACT.Ln, bias=eps[:, 0:1])\
                            .then_inc(S["group_log"], 1)
                if norm:
                    N1.log_var(nc, act, i + 2, eps)
                if chan:
                    for c in range(CT):
                        act.wait_ge(S["group_log"], CT * i + c + 1)
                        nc.scalar.activation(yc[:, c, :], sq[:, c, :], ACT.Exp, scale=-0.5)\
                            .then_inc(S["group_rstd"], 1)
                if norm:
                    N1.inverse_std(nc, act, i + 2)
                if project:
                    for name in ("dec2", "r", "v"):
                        for c in range(CT):
                            take(i + 1, name, c)
                if chan:
                    N2.log_var(nc, act, i, eps)
                    N2.inverse_std(nc, act, i)

            def gate(i, c):
                act.wait_ge(S["gate_product"], CT * i + c + 1)
                nc.scalar.activation(g[:, c, :], gate_bank[:, :], ACT.Sigmoid).then_inc(S["gate_sigmoid"], 1)

            def during(i, recur, chan, mix):
                if mix:
                    if recur:
                        act.wait_ge(S["input_mixed"], NM * (i + 2))
                    affine(N1, i + 2, "ln1_w", "ln1_b", mix_banks)
                if recur:
                    if chan:
                        act.wait_ge(S["gated"], CT * (i + 1))
                    gate(i + 1, 0)
                if chan:
                    affine(N2, i, "ln2_w", "ln2_b", c_banks)
                if recur:
                    gate(i + 1, 1)
                if mix:
                    act.wait_ge(S["low_product"], 2 * (i + 2) + 1)
                    nc.scalar.activation(low1[:, :], mix_banks[0][:, :], ACT.Tanh).then_inc(S["low_tanh"], 1)
                    act.wait_ge(S["low_product"], 2 * (i + 2) + 2)
                    nc.scalar.activation(low2[:, :], mix_banks[1][0:MD, :], ACT.Tanh).then_inc(S["low_tanh"], 1)
                if chan:
                    for c in range(CT):
                        act.wait_ge(S["key_product"], CT * i + c + 1)
                        nc.scalar.activation(kk[:, c, :], c_banks[c][:, :], ACT.Relu).then_inc(S["key_relu"], 1)
                    for c in range(CT):
                        act.wait_ge(S["key_relu"], CT * i + c + 1)
                        nc.scalar.activation(kk[:, c, :], kk[:, c, :], ACT.Square).then_inc(S["key_squared"], 1)
                    for b in range(2):
                        act.wait_ge(S["receptance_product"], 2 * i + b + 1)
                        nc.scalar.activation(rr[:, b, :], c_banks[b][:, :], ACT.Sigmoid)\
                            .then_inc(S["receptance_sigmoid"], 1)

            schedule(act, between, during)

        @block.tensor
        def _(pe):
            pe.wait_ge(S["constants_rounded"], 1)

            def turn(N, i, at):
                for c in range(CT):
                    for j in range(TT):
                        if c == 0:
                            pe.wait_ge(N.normalised, TT * i + j + 1)
                        ins = nc.tensor.transpose(at[c][:, j * P:(j + 1) * P], N.xh[:, j, c * P:(c + 1) * P], ident)
                    ins.then_inc(N.turned, 1)

            def product(bank, w, src, co):
                for ci in range(CT):
                    ins = nc.tensor.matmul(bank, w[:, ci, co], src[:, ci, :], start=ci == 0, stop=ci == CT - 1)
                return ins

            def token_product(b, w, src):
                for j in range(2):
                    tok = slice((2 * b + j) * P, (2 * b + j + 1) * P)
                    for ci in range(CT):
                        ins = nc.tensor.matmul(c_banks[b][:, j * C:(j + 1) * C], src[:, ci, tok], w[:, ci, :],
                                               start=ci == 0, stop=ci == CT - 1)
                return ins

            def mix_product(i, n):
                j, c = MIX[n]
                if n < 2:
                    pe.wait_ge(S["low_tanh"], 2 * i + n + 1)
                else:
                    pe.wait_ge(S["mix_difference"], NM * i + (n - 1))
                w, src, at = (maa_w2g, low2, 0) if j == 4 else (maa_w2, low1, MD * j)
                nc.tensor.matmul(mix_banks[n % 2][:, :], w[at:at + MD, c * P:(c + 1) * P], src[at:at + MD, :],
                                 start=True, stop=True).then_inc(S["mix_product"], 1)

            def project_item(i, name, c):
                n = AT[name, c]
                if n >= 4:
                    pe.wait_ge(S["projection_taken"], NP * i + (n - 3))
                elif n < 2:
                    pe.wait_ge(S["mix_difference"], NM * i + (NM - 1 + n))
                bank = proj_banks[n % 4]
                if name == "dec2":
                    pe.wait_ge(S["projection_taken"], NP * i + 1)
                    ins = nc.tensor.matmul(bank[:, :], decay_w2[0:DD, c * P:(c + 1) * P], dh[:, :],
                                           start=True, stop=True)
                elif name == "q":
                    pe.wait_ge(S["ruk_ready"], CT * i + c + 1)
                    nc.tensor.matmul(bank[:, :], ones8, qv[:, c, :], start=True, stop=True)\
                        .then_inc(S["ruk_summed"], 1)
                    return
                else:
                    j = SRC[name]
                    pe.wait_ge(S["input_mixed"], NM * i + CT * (MIX_ORDER.index(j) + 1))
                    if name == "dec1":
                        ins = product(bank[0:DD, :], decay_w1, xj[j], slice(0, DD))
                    else:
                        ins = product(bank[:, :], W["W" + name], xj[j], slice(c * P, (c + 1) * P))
                ins.then_inc(S["projected"], 1)

            def spread_v(i, n):
                c, t = STEPS[n]
                if n >= VRING:
                    pe.wait_ge(S["kv_ready"], NS * i + (n - VRING + 1))
                if t == 0:
                    pe.wait_ge(S["v_low"], CT * i + c + 1)
                bank = v_banks[n % VRING]
                nc.tensor.matmul(bank[:, :], spread[:, t, :], vhi[:, c, :], start=True, stop=False)
                nc.tensor.matmul(bank[:, :], spread[:, t, :], vlo[:, c, :], start=False, stop=True)\
                    .then_inc(S["v_spread"], 1)

            def sum_rs(i, n):
                c, t = STEPS[n]
                pe.wait_ge(S["rs_ready"], NS * i + n + 1)
                if c == 1 and t == 0:
                    pe.wait_ge(S["gate_ready"], CT * (i + 1))
                nc.tensor.matmul(y_banks[c][:, :], gather[:, t, :], rs[:, n % RING, :], start=t == 0,
                                 stop=t == HS - 1).then_inc(S["rs_summed"], 1)

            def between(i, project, chan, norm):
                if project:
                    project_item(i + 1, "dec1", 0)
                if chan:
                    for c in range(CT):
                        pe.wait_ge(S["heads_out"], CT * i + c + 1)
                        nc.tensor.matmul(c_banks[c][:, :], centre8, yc[:, c, :], start=True, stop=True)\
                            .then_inc(S["centred"], 1)
                if project:
                    project_item(i + 1, "k", 0)
                    project_item(i + 1, "k", 1)
                if chan:
                    for c in range(CT):
                        pe.wait_ge(S["squared"], CT * i + c + 1)
                        nc.tensor.matmul(y_banks[c][:, :], mean8, sq[:, c, :], start=True, stop=True)\
                            .then_inc(S["group_var"], 1)
                if project:
                    for name in ("dec2", "r", "v", "q"):
                        for c in range(CT):
                            project_item(i + 1, name, c)
                if chan:
                    pe.wait_ge(S["gated"], CT * (i + 1))
                    for b in range(2):
                        token_product(b, W["Wo"], yc).then_inc(S["output_product"], 1)

            def during(i, recur, chan, mix):
                if recur:
                    spread_v(i + 1, 0)
                    pe.wait_ge(S["own_part_ready"], CT * (i + 2))
                    spread_v(i + 1, 1)
                if mix:
                    turn(N1, i + 2, mix_banks)
                for n in range(NS):
                    if recur and n + VRING < NS:
                        spread_v(i + 1, n + VRING)
                    if recur and n in GATE_STEPS:
                        c = GATE_STEPS.index(n)
                        pe.wait_ge(S["input_mixed"], NM * (i + 2))
                        if c > 0:
                            pe.wait_ge(S["gate_ready"], CT * (i + 1) + c)
                        product(gate_bank[:, :], W["Wg"], xj[SRC["g"]], slice(c * P, (c + 1) * P))\
                            .then_inc(S["gate_product"], 1)
                    if chan and n == 2:
                        turn(N2, i, c_banks)
                    if mix and n == 4:
                        pe.wait_ge(S["low_input"], CT * (i + 3))
                        product(mix_banks[0][:, :], maa_w1, xx, slice(0, P)).then_inc(S["low_product"], 1)
                    if mix and n == 5:
                        product(mix_banks[1][0:MD, :], maa_w1, xx, slice(P, P + MD)).then_inc(S["low_product"], 1)
                    if mix and 0 <= n - 6 < NM:
                        mix_product(i + 2, n - 6)
                    if chan and n in (8, 9):
                        c = n - 8
                        pe.wait_ge(S["key_input"], CT * (i + 1))
                        product(c_banks[c][:, :], W["fWk"], fx[0], slice(c * P, (c + 1) * P))\
                            .then_inc(S["key_product"], 1)
                    if chan and n in (10, 11):
                        b = n - 10
                        pe.wait_ge(S["receptance_input"], CT * (i + 1))
                        pe.wait_ge(S["key_relu"], CT * i + b + 1)
                        token_product(b, W["fWr"], fx[1]).then_inc(S["receptance_product"], 1)
                    if chan and n in (14, 15):
                        b = n - 14
                        pe.wait_ge(S["key_squared"], CT * (i + 1))
                        pe.wait_ge(S["receptance_sigmoid"], 2 * i + b + 1)
                        token_product(b, W["fWv"], kk).then_inc(S["value_product"], 1)
                    if recur and n > 0:
                        sum_rs(i + 1, n - 1)
                if recur:
                    sum_rs(i + 1, NS - 1)

            schedule(pe, between, during)


def constants():
    p = np.arange(P)
    head = p[:, None] // HS == p[None, :] // HS
    spread = np.stack([(head & (p[:, None] % HS == t)) for t in range(HS)], 1).astype(np.float32)
    gather = np.stack([(head & (p[None, :] % HS == t)) for t in range(HS)], 1).astype(np.float32)
    head = head.astype(np.float32)
    return {"ones8": head,
            "mean8": head / np.float32(HS), "centre8": np.eye(P, dtype=np.float32) - head / np.float32(HS),
            "spread": spread.reshape(P, -1), "gather": gather.reshape(P, -1)}


def constants0():
    p = np.arange(P)
    sample = (p[:, None] // CC == p[None, :] // CC).astype(np.float32)
    pick = np.stack([np.broadcast_to((p // CC == s)[:, None], (P, P)) for s in range(2)], 1).astype(np.float32)
    return {"mean64": sample / np.float32(CC), "pick": pick.reshape(P, -1) / np.float32(CC),
            "ident": np.eye(P, dtype=np.float32)}


def tiles(a):
    return a.reshape(-1, P, a.shape[1]).transpose(1, 0, 2).reshape(P, -1)


def pack0(inputs):
    def l0(name):
        return np.asarray(inputs["L0_xattn_" + name])

    def twice(a):
        return np.concatenate([a, a], 0)

    def doubled(w):
        return tiles(np.concatenate([w, w], 1))

    f = {"wqn": doubled(l0("Wq")), "wkn": doubled(l0("Wkv")[:HP * P]), "wvn": doubled(l0("Wkv")[HP * P:]),
         "bq": l0("bq").reshape(HP, P).T, "wo": tiles(l0("Wo").T), "bv": l0("bkv")[HP * P:].reshape(HP, P).T,
         "gamma": twice(l0("gamma")[:, None]), "beta": twice(l0("beta")[:, None]), "bo": twice(l0("bo")[:, None]),
         **constants0()}
    return np.ascontiguousarray(np.concatenate([f[name] for name, _ in FIELDS0], 1))


def pack(inputs):
    def l1(name):
        return np.asarray(inputs["L1_xattn_" + name])

    def padded(a):
        full = np.zeros((P, a.shape[1]), a.dtype)
        full[:a.shape[0]] = a
        return full

    f = {"maa_w1": tiles(l1("maa_w1")), "maa_w2": l1("maa_w2")[:4].reshape(P, C), "maa_w2g": padded(l1("maa_w2")[4]),
         "decay_w1": tiles(l1("decay_w1")), "decay_w2": padded(l1("decay_w2")), **constants()}
    for name in VECTORS:
        f[name] = l1(name).reshape(CT, P).T
    for name in SQUARES:
        f[name] = tiles(l1(name).T)
    return np.ascontiguousarray(np.concatenate([f[name] for name, _ in FIELDS], 1))


def kernel(**inputs):
    import concourse.bacc as bacc
    from concourse.bass_utils import run_bass_kernel_spmd

    x = np.ascontiguousarray(np.asarray(inputs["x"]))
    context = np.ascontiguousarray(np.asarray(inputs["ctx_2048"]))
    shift = np.ascontiguousarray(context[:, 0:2].reshape(B, 2, CT, P).transpose(3, 1, 2, 0))
    state = np.ascontiguousarray(context[:, 2:2 + HS].reshape(B, CT, P, HS).transpose(2, 1, 3, 0))
    arrays = {"x_dram": x, "ctx_dram": context, "params_dram": pack(inputs), "params0_dram": pack0(inputs),
              "shift_dram": shift, "state_dram": state}

    nc = bacc.Bacc("TRN2", target_bir_lowering=False, num_devices=1)
    aps = {n: nc.dram_tensor(n, v.shape, FP32, kind="ExternalInput").ap() for n, v in arrays.items()}
    out = nc.dram_tensor("out_dram", (PAIRS, P, C), FP32, kind="ExternalOutput").ap()
    build(nc, aps["x_dram"].rearrange("(a s) l n -> (s l) a n", s=2), aps["x_dram"], aps["ctx_dram"],
          aps["params_dram"], aps["params0_dram"], aps["shift_dram"], aps["state_dram"],
          out.rearrange("a p n -> p a n"))
    result = run_bass_kernel_spmd(nc, [arrays], core_ids=[0])
    return np.asarray(result.results[0]["out_dram"]).reshape(B, L, C)
```
